# Optimizing a Trainium2 kernel written in Bass

```python
import numpy as np
import jax
import jax.numpy as jnp

def _softmax(x, axis=-1):
    return jax.nn.softmax(x, axis=axis)

def _gelu(x):
    return jax.nn.gelu(x, approximate=True)

def _silu(x):
    return jax.nn.silu(x)

def _sigmoid(x):
    return jax.nn.sigmoid(x)

def _layernorm(x, axis=-1, eps=1e-05):
    m = jnp.mean(x, axis=axis, keepdims=True)
    v = jnp.var(x, axis=axis, keepdims=True)
    return (x - m) / jnp.sqrt(v + eps)

def _scatter_add(tgt, idx, src, axis=0):
    return tgt.at[idx].add(src)

def _segment_sum(src, seg, n):
    return jax.ops.segment_sum(src, seg, n)
kernel_name = 'mk_macaron_d1_jaxref_r4_a49bb4'

def setup_inputs(seed: int=0):
    np.random.seed(seed)
    _w = jnp.asarray

    def _L0_attn_setup():
        import jax, jax.numpy as jnp
        import numpy as np
        B, T, D, H = (4, 512, 256, 16)
        HD = D // H
        EPS = 1e-05
        NEG = 10000000000.0
        key = jax.random.key(seed)
        k1, k2, k3 = jax.random.split(key, 3)
        return {'target': jax.random.normal(k1, (B, T, D), dtype=jnp.float32), 'w_qkv': jax.random.normal(k2, (D, 3 * D), dtype=jnp.float32) * 0.02, 'w_proj': jax.random.normal(k3, (D, D), dtype=jnp.float32) * (0.02 / np.sqrt(24.0)), 'b_proj': jnp.zeros((D,), dtype=jnp.float32), 'ln_gamma': jnp.ones((D,), dtype=jnp.float32), 'ln_beta': jnp.zeros((D,), dtype=jnp.float32)}
    _L0_attn_in = _L0_attn_setup()

    def _L0_ffn_setup():
        import jax, jax.numpy as jnp
        import numpy as np
        B, T, D_IN, D_OUT = (4, 512, 256, 256)
        N_EXPERTS, N_ACTIVE = (8, 2)
        key = jax.random.key(seed)
        k1, k2, k3, k4, k5 = jax.random.split(key, 5)
        s_in = 1.0 / np.sqrt(D_IN)
        x = jax.random.normal(k1, (B, T, D_IN), dtype=jnp.float32)
        w_router = jax.random.uniform(k2, (N_EXPERTS, D_IN), jnp.float32, -s_in, s_in)
        b_router = jax.random.uniform(k3, (N_EXPERTS,), jnp.float32, -s_in, s_in)
        w_experts = jax.random.uniform(k4, (N_EXPERTS, D_OUT, D_IN), jnp.float32, -s_in, s_in)
        b_experts = jax.random.uniform(k5, (N_EXPERTS, D_OUT), jnp.float32, -s_in, s_in)
        return {'x': x, 'w_router': w_router, 'b_router': b_router, 'w_experts': w_experts, 'b_experts': b_experts}
    _L0_ffn_in = _L0_ffn_setup()
    _d = {'L0_attn_target': _L0_attn_in['target'], 'L0_attn_w_qkv': _L0_attn_in['w_qkv'], 'L0_attn_w_proj': _L0_attn_in['w_proj'], 'L0_attn_b_proj': _L0_attn_in['b_proj'], 'L0_attn_ln_gamma': _L0_attn_in['ln_gamma'], 'L0_attn_ln_beta': _L0_attn_in['ln_beta'], 'L0_ffn_w_router': _L0_ffn_in['w_router'], 'L0_ffn_b_router': _L0_ffn_in['b_router'], 'L0_ffn_w_experts': _L0_ffn_in['w_experts'], 'L0_ffn_b_experts': _L0_ffn_in['b_experts']}
    _x0 = _d['L0_attn_target']
    _d['L0_attn_target'] = jax.random.normal(jax.random.fold_in(jax.random.key(seed), 1), (4, 1024, 256), dtype=_x0.dtype)
    del _x0
    return _d

def reference(L0_attn_target, L0_attn_w_qkv, L0_attn_w_proj, L0_attn_b_proj, L0_attn_ln_gamma, L0_attn_ln_beta, L0_ffn_w_router, L0_ffn_b_router, L0_ffn_w_experts, L0_ffn_b_experts):

    def _L0_attn_ref(target, w_qkv, w_proj, b_proj, ln_gamma, ln_beta):
        import jax, jax.numpy as jnp
        import numpy as np
        B, T, D, H = (4, 512, 256, 16)
        HD = D // H
        EPS = 1e-05
        NEG = 10000000000.0
        b, t, d = target.shape
        resid = target
        qkv = target @ w_qkv
        q, k, v = jnp.split(qkv, 3, axis=-1)
        q = q.reshape(b, t, H, HD).transpose(0, 2, 1, 3)
        k = k.reshape(b, t, H, HD).transpose(0, 2, 1, 3)
        v = v.reshape(b, t, H, HD).transpose(0, 2, 1, 3)
        scores = jnp.einsum('bhqd,bhkd->bhqk', q, k) * (1.0 / np.sqrt(HD))
        causal = (jnp.arange(t)[:, None] >= jnp.arange(t)[None, :]).astype(scores.dtype)
        scores = scores * causal - (1.0 - causal) * NEG
        attn = jax.nn.softmax(scores, axis=-1)
        out = jnp.einsum('bhqk,bhkd->bhqd', attn, v)
        out = out.transpose(0, 2, 1, 3).reshape(b, t, d)
        proj = out @ w_proj + b_proj
        x = proj + resid
        mu = jnp.mean(x, axis=-1, keepdims=True)
        var = jnp.var(x, axis=-1, keepdims=True)
        return (x - mu) * jax.lax.rsqrt(var + EPS) * ln_gamma + ln_beta

    def _L0_ffn_ref(x, w_router, b_router, w_experts, b_experts):
        import jax, jax.numpy as jnp
        import numpy as np
        B, T, D_IN, D_OUT = (4, 512, 256, 256)
        N_EXPERTS, N_ACTIVE = (8, 2)
        gamma = jax.nn.softmax(jnp.einsum('btd,ed->bte', x, w_router) + b_router, axis=-1)
        _, expert_ids = jax.lax.top_k(gamma, N_ACTIVE)
        mask = (expert_ids[..., None] == jnp.arange(N_EXPERTS)).any(axis=-2)
        y_all = jnp.einsum('btd,eod->bteo', x, w_experts) + b_experts
        y = jnp.einsum('bte,bteo->bto', mask.astype(x.dtype), y_all)
        return y
    x = L0_attn_target
    x = x + 0.5 * _L0_ffn_ref(_layernorm(x, axis=-1), L0_ffn_w_router, L0_ffn_b_router, L0_ffn_w_experts, L0_ffn_b_experts)
    x = x + _L0_attn_ref(_layernorm(x, axis=-1), L0_attn_w_qkv, L0_attn_w_proj, L0_attn_b_proj, L0_attn_ln_gamma, L0_attn_ln_beta)
    x = x + 0.5 * _L0_ffn_ref(_layernorm(x, axis=-1), L0_ffn_w_router, L0_ffn_b_router, L0_ffn_w_experts, L0_ffn_b_experts)
    return x

_drawn_inputs = setup_inputs


def setup_inputs(seed=0):
    import zlib

    import numpy as np

    out = dict(_drawn_inputs(seed))
    spreads = {'L0_attn_b_proj': (0.0, 0.1),
     'L0_attn_ln_gamma': (1.0, 0.2),
     'L0_attn_ln_beta': (0.0, 0.1)}
    factors = {'L0_attn_w_qkv': 8.0, 'L0_attn_w_proj': 8.0}
    for name, (base, spread) in spreads.items():
        noise = np.random.default_rng([zlib.crc32(name.encode()), seed]).standard_normal(out[name].shape)
        drawn = base * np.exp(spread * noise) if base else spread * noise
        out[name] = jnp.asarray(drawn.astype(out[name].dtype))
    for name, factor in factors.items():
        out[name] = (out[name] * factor).astype(out[name].dtype)
    return out
```

```python
from contextlib import ExitStack

import concourse.bass as bass
from concourse import mybir

F32 = mybir.dt.float32
F32R = mybir.dt.float32r
BF16 = mybir.dt.bfloat16
ALU = mybir.AluOpType
ACT = mybir.ActivationFunctionType
AX = mybir.AxisListType
ds = bass.ds

P = 128
BATCH, SEQ, D = 4, 1024, 256
TOK = BATCH * SEQ
NT = TOK // P
DK = D // P
NE = 8
HEADS, HD = 16, 16
CH = 512
TPC = CH // P
NCH = TOK // CH
EPS = 1e-5

GH = 4
HGS = HEADS // GH
NG = BATCH * HGS
KT = SEQ // P
SLOT = 32
SCALE = HD ** -0.5
MASKED = -1.0e30
ROWS = 6 * HD
MROWS = ROWS + 3
PARTS = ((0, 3), (3, 2), (5, 1))

CREDIT = 8


def at(events):
    return max(events, 0) + CREDIT if isinstance(events, int) else events + CREDIT


class Group:

    def __init__(self, turn, u):
        self.turn, self.u = turn, u
        self.n = 3 * turn + u

    def __add__(self, k):
        return Group(self.turn + (self.u + k) // 3, (self.u + k) % 3)


class Signals:
    pass


class Shared:
    pass


def build(nc, x, w_qkv, w_proj, b_proj, ln_gamma, ln_beta, w_router, b_router, w_experts, b_experts, out):
    s = Shared()
    s.x_in = x.rearrange("b (t p) d -> p (b t) d", p=P)
    s.out = out.rearrange("b (t p) d -> p (b t) d", p=P)
    s.q_parts = nc.dram_tensor("q_parts", (3, D, TOK), BF16).ap()
    s.k_parts = nc.dram_tensor("k_parts", (3, D, TOK), BF16).ap()
    s.att_num = nc.dram_tensor("att_num", (D, TOK), F32).ap()
    s.att_rec = nc.dram_tensor("att_rec", (HEADS, TOK), F32).ap()
    with ExitStack() as ctx:
        def sb(name, shape, dt=F32, scope=ctx):
            return scope.enter_context(nc.sbuf_tensor(name, shape, dt))

        s.xs = sb("xs", [P, NT, D])
        s.ln2 = sb("ln2", [P, NT, 2])
        s.ident = sb("ident", [P, P])
        s.ident_b = sb("ident_b", [P, P], BF16)
        s.eps = sb("eps", [P, 1])
        s.wp = sb("wp", [P, DK, D])
        s.gamma = sb("gamma", [P, D])
        s.beta = sb("beta", [P, D])
        s.bproj = sb("bproj", [P, D])
        s.brouter = sb("brouter", [NE, 1])
        s.before = sb("before", [P, TPC * NE, NE])
        s.wr = [sb(f"wr{n}", [P, DK, NE], F32R) for n in range(2)]
        s.we = [sb(f"we{n}", [P, DK, NE * D], F32R) for n in range(2)]
        s.bias_rows = sb("bias_rows", [P, TPC, D], BF16)
        with ExitStack() as front:
            s.v_all = sb("v_all", [P, NT, D], F32, front)
            with ExitStack() as early:
                s.wqk = [sb(f"wqk{n}", [P, DK, 2 * D], F32R, early) for n in range(2)]
                s.wv = sb("wv", [P, DK, D], F32, early)
                setup(nc, s, w_qkv, w_proj, b_proj, ln_gamma, ln_beta, w_router, b_router, w_experts, b_experts)
                ffn_phase(nc, s, True)
            attention_phase(nc, s)
        ffn_phase(nc, s, False)


def setup(nc, s, w_qkv, w_proj, b_proj, ln_gamma, ln_beta, w_router, b_router, w_experts, b_experts):
    with ExitStack() as ctx:
        def sb(name, shape, dt=F32):
            return ctx.enter_context(nc.sbuf_tensor(name, shape, dt))

        def sem(name):
            return ctx.enter_context(nc.semaphore(name))

        we_in = sb("we_in", [P, NE * DK, D])
        wr_in = sb("wr_in", [NE, D])
        wqk_in = sb("wqk_in", [P, DK, 2 * D])
        be_in = sb("be_in", [NE, D])
        be_rest = sb("be_rest", [NE, D])
        be_part = sb("be_part", [NE, 3, D], BF16)
        pt = [ctx.enter_context(nc.psum_tensor(f"setup_t{n}", [P, CH], F32)) for n in range(4)]
        x_loaded, we_loaded, small_loaded = sem("x_loaded"), sem("we_loaded"), sem("small_loaded")
        consts, bias_zero, bias_step, bias_placed = sem("consts"), sem("bias_zero"), sem("bias_step"), sem("bias_placed")
        turned, hi_done, lo_done, wqk_hi = sem("w_turned"), sem("w_hi_done"), sem("w_lo_done"), sem("wqk_hi")
        nblk = DK * NE * D // CH
        small = 9
        with nc.Block() as block:
            @block.sync
            def _(sp):
                sp.dma_start(we_in[:], w_experts.rearrange("e (h p) d -> p (e h) d", p=P)).then_inc(we_loaded, 16)
                sp.dma_start(s.xs[:], s.x_in).then_inc(x_loaded, 16)
                sp.wait_ge(bias_zero, 1)
                sp.wait_ge(bias_step, 4)
                for t in range(TPC):
                    for part in range(3):
                        row = 32 * t + NE * part
                        sp.dma_start(s.bias_rows[row:row + NE, t, :], be_part[:, part, :]).then_inc(bias_placed, 16)
                sp.wait_ge(bias_placed, 16 * 3 * TPC)
                sp.wait_ge(x_loaded, 16)

            @block.scalar
            def _(act):
                act.dma_start(wr_in[:], w_router).then_inc(small_loaded, 16)
                act.dma_start(be_in[:], b_experts).then_inc(small_loaded, 16)
                act.dma_start(wqk_in[:], w_qkv[:, 0:2 * D].rearrange("(k p) n -> p k n", p=P)).then_inc(small_loaded, 16)
                act.dma_start(s.wv[:], w_qkv[:, 2 * D:3 * D].rearrange("(k p) n -> p k n", p=P)).then_inc(small_loaded, 16)
                act.dma_start(s.wp[:], w_proj.rearrange("(k p) n -> p k n", p=P)).then_inc(small_loaded, 16)
                act.dma_start(s.brouter[:], b_router.rearrange("(e a) -> e a", a=1)).then_inc(small_loaded, 16)
                for row, full in ((b_proj, s.bproj), (ln_gamma, s.gamma), (ln_beta, s.beta)):
                    act.dma_start(full[:], row.rearrange("(a d) -> a d", a=1).broadcast_to([P, D])).then_inc(small_loaded, 16)
                act.wait_ge(small_loaded, 16 * small)
                act.activation(s.wqk[0][:], wqk_in[:], ACT.Copy).then_inc(wqk_hi, 1)
                for b in range(nblk):
                    half, j = divmod(b, nblk // DK)
                    act.wait_ge(turned, b + 1)
                    act.activation(s.we[0][:, half, j * CH:(j + 1) * CH], pt[b % 4][:], ACT.Copy).then_inc(hi_done, 1)
                act.wait_ge(turned, nblk + 1)
                act.activation(s.wr[0][:].rearrange("p k e -> p (k e)"), pt[nblk % 4][:, 0:DK * NE],
                               ACT.Copy).then_inc(hi_done, 1)

            @block.gpsimd
            def _(pool):
                pool.memset(s.ident[:], 0.0).then_inc(consts, 1)
                pool.memset(s.before[:], 1.0).then_inc(consts, 1)
                pool.memset(s.eps[:], EPS).then_inc(consts, 1)
                pool.memset(s.bias_rows[:], 0.0).then_inc(bias_zero, 1)
                pool.wait_ge(consts, 3)
                pool.affine_select(out=s.ident[:], in_=s.ident[:], compare_op=ALU.not_equal, fill=1.0, base=0,
                                   pattern=[[-1, P]], channel_multiplier=1).then_inc(consts, 1)
                before = s.before[:].rearrange("p (t e) f -> p t e f", e=NE)
                pool.affine_select(out=before, in_=before, compare_op=ALU.is_gt, fill=0.0, base=0,
                                   pattern=[[0, TPC], [1, NE], [-1, NE]], channel_multiplier=0).then_inc(consts, 1)

            @block.tensor
            def _(pe):
                pe.wait_ge(consts, 5)
                pe.wait_ge(we_loaded, 16)
                for b in range(nblk):
                    half, j = divmod(b, nblk // DK)
                    if b >= 4:
                        pe.wait_ge(lo_done, b - 3)
                    for i in range(4):
                        last = nc.tensor.transpose(pt[b % 4][:, i * P:(i + 1) * P],
                                                   we_in[:, 4 * j + i, half * P:(half + 1) * P], s.ident[:])
                    last.then_inc(turned, 1)
                pe.wait_ge(small_loaded, 16 * small)
                pe.wait_ge(lo_done, nblk - 3)
                for half in range(DK):
                    last = nc.tensor.transpose(pt[nblk % 4][:, half * NE:(half + 1) * NE],
                                               wr_in[:, half * P:(half + 1) * P], s.ident[0:NE, 0:NE])
                last.then_inc(turned, 1)

            @block.vector
            def _(dve):
                dve.wait_ge(consts, 5)
                dve.tensor_copy(s.ident_b[:], s.ident[:])
                for b in range(nblk):
                    half, j = divmod(b, nblk // DK)
                    cols = slice(j * CH, (j + 1) * CH)
                    dve.wait_ge(hi_done, b + 1)
                    dve.tensor_tensor(s.we[1][:, half, cols], pt[b % 4][:], s.we[0][:, half, cols].bitcast(F32),
                                      ALU.subtract).then_inc(lo_done, 1)
                dve.wait_ge(hi_done, nblk + 1)
                dve.tensor_tensor(s.wr[1][:].rearrange("p k e -> p (k e)"), pt[nblk % 4][:, 0:DK * NE],
                                  s.wr[0][:].rearrange("p k e -> p (k e)").bitcast(F32), ALU.subtract)
                dve.wait_ge(small_loaded, 16 * small)
                dve.wait_ge(wqk_hi, 1)
                dve.tensor_tensor(s.wqk[1][:], wqk_in[:], s.wqk[0][:].bitcast(F32), ALU.subtract)
                dve.tensor_copy(be_part[:, 0, :], be_in[:]).then_inc(bias_step, 1)
                dve.wait_ge(bias_step, 1)
                dve.tensor_tensor(be_rest[:], be_in[:], be_part[:, 0, :], ALU.subtract).then_inc(bias_step, 1)
                dve.wait_ge(bias_step, 2)
                dve.tensor_copy(be_part[:, 1, :], be_rest[:]).then_inc(bias_step, 1)
                dve.wait_ge(bias_step, 3)
                dve.tensor_tensor(be_part[:, 2, :], be_rest[:], be_part[:, 1, :], ALU.subtract).then_inc(bias_step, 1)


def ffn_phase(nc, s, first):
    with ExitStack() as ctx:
        tag = "a" if first else "c"

        def sb(name, shape, dt=F32):
            return ctx.enter_context(nc.sbuf_tensor(f"{tag}_{name}", shape, dt))

        every = []

        def sem(name):
            every.append(ctx.enter_context(nc.semaphore(f"{tag}_{name}")))
            return every[-1]

        q = Signals()
        q.normed_stats, q.normed_aggr, q.std_done = sem("normed_stats"), sem("normed_aggr"), sem("std_done")
        q.rstd_done, q.norm_ready, q.xh_ready = sem("rstd_done"), sem("norm_ready"), sem("xh_ready")
        q.turned, q.hi_ready, q.lo_ready = sem("turned"), sem("hi_ready"), sem("lo_ready")
        q.router_done, q.logits_ready, q.logits_turned = sem("router_done"), sem("logits_ready"), sem("logits_turned")
        q.logits_copied, q.rank_step, q.mask_ready = sem("logits_copied"), sem("rank_step"), sem("mask_ready")
        q.mask_zero, q.mask_turned, q.maskt_ready = sem("mask_zero"), sem("mask_turned"), sem("maskt_ready")
        q.bias_done, q.bias_ready = sem("bias_done"), sem("bias_ready")
        q.ffn_bank, q.combined, q.x_ready = sem("ffn_bank"), sem("combined"), sem("x_ready")
        q.apart = sem("apart")
        if first:
            q.st2, q.aggr2, q.std2, q.rstd2, q.norm2 = sem("st2"), sem("aggr2"), sem("std2"), sem("rstd2"), sem("norm2")
            q.xh2_ready, q.turned2, q.hi2_ready, q.lo2_ready = sem("xh2_ready"), sem("turned2"), sem("hi2_ready"), sem("lo2_ready")
            q.v_bank, q.v_ready, q.qk_bank = sem("v_bank"), sem("v_ready"), sem("qk_bank")
            q.qk_hi, q.qk_rest, q.qk_mid, q.qk_lo = sem("qk_hi"), sem("qk_rest"), sem("qk_mid"), sem("qk_lo")
            q.stored = [sem(f"stored{j}") for j in range(4)]
        else:
            q.num_loaded0, q.num_loaded1, q.att_ready = sem("num_loaded0"), sem("num_loaded1"), sem("att_ready")
            q.proj_bank, q.resid_ready, q.resid_bias, q.xa_ready = sem("proj_bank"), sem("resid_ready"), sem("resid_bias"), sem("xa_ready")
            q.st3, q.aggr3, q.std3, q.rstd3, q.norm3 = sem("st3"), sem("aggr3"), sem("std3"), sem("rstd3"), sem("norm3")
            q.y_ready, q.scaled, q.x_shifted, q.x2_ready = sem("y_ready"), sem("scaled"), sem("x_shifted"), sem("x2_ready")
            q.written = sem("written")

        st = sb("st", [P, TPC, 6])
        mv = sb("mv", [P, TPC, 2])
        std = sb("std", [P, TPC, 1])
        ln = sb("ln", [P, TPC, 2])
        xh = sb("xh", [P, TPC, D])
        xt = [[sb(f"xt{par}{n}", [P, DK, CH], F32R) for n in range(2)] for par in range(2)]
        logits_t = sb("logits_t", [NE, CH])
        logits = sb("logits", [P, TPC * NE])
        gt = sb("gt", [P, TPC * NE, NE])
        eq = sb("eq", [P, TPC * NE, NE])
        wins = sb("wins", [P, TPC * NE, NE])
        rank = sb("rank", [P, TPC * NE])
        mask = [sb(f"mask{par}", [P, TPC, 32], BF16) for par in range(2)]
        mask_t = [sb(f"mask_t{par}", [P, P], BF16) for par in range(2)]
        ybias = [sb(f"ybias{pair}", [P, 2, D]) for pair in range(2)]
        acc = [[sb(f"acc{par}{n}", [P, D]) for n in range(2)] for par in range(2)]
        ring = [ctx.enter_context(nc.psum_tensor(f"{tag}_ring{n}", [P, CH], F32)) for n in range(4)]
        pt = [ctx.enter_context(nc.psum_tensor(f"{tag}_pt{n}", [P, CH], F32)) for n in range(2)]
        pr = ctx.enter_context(nc.psum_tensor(f"{tag}_pr", [P, CH], F32))
        pb = ctx.enter_context(nc.psum_tensor(f"{tag}_pb", [P, CH], F32))
        pr_b = pr[:, 0:P // 2].bitcast(BF16)
        if first:
            st2, mv2, std2 = sb("st2", [P, TPC, 6]), sb("mv2", [P, TPC, 2]), sb("std2", [P, TPC, 1])
            xh2 = sb("xh2", [P, TPC, D])
            xt2 = sb("xt2", [P, DK, CH])
            xt2r = [sb(f"xt2r{n}", [P, DK, CH], F32R) for n in range(2)]
            part = [sb(f"part{n}", [P, 3, CH], BF16) for n in range(4)]
            rest = [sb(f"rest{n}", [P, CH]) for n in range(2)]
        else:
            num = [sb(f"num{par}", [P, DK, CH]) for par in range(2)]
            rec = [sb(f"rec{par}", [P, DK, CH]) for par in range(2)]
            att = [sb(f"att{par}", [P, DK, CH]) for par in range(2)]
            st3, mv3, std3, ln3 = sb("st3", [P, TPC, 6]), sb("mv3", [P, TPC, 2]), sb("std3", [P, TPC, 1]), sb("ln3", [P, TPC, 2])
            resid = sb("resid", [P, TPC, D])
            residb = sb("residb", [P, TPC, D])
            xa = sb("xa", [P, TPC, D])
            yn = sb("yn", [P, TPC, D])
            yg = sb("yg", [P, TPC, D])
            xb = sb("xb", [P, TPC, D])

        pairs = 2
        last_slot = NCH if first else NCH - 1

        def slots(engine, slot):
            slot(0, 0, 0)
            with engine.Fori(0, pairs) as i:
                for u in range(1, 3):
                    slot(2 * i + u, u % 2, i + u // 2)
            for c in range(1 + 2 * pairs, last_slot + 1):
                slot(c, c % 2, c // 2)

        def exists(c):
            return not isinstance(c, int) or 0 <= c < NCH

        def tiles(c):
            return ds(TPC * c, TPC)

        def norm_stats(dve, src, m, st_, mv_, std_, out_ln, n_st, n_ag, n_sd, n_rc, n_rd):
            for t in range(TPC):
                last = dve.bn_stats(st_[:, t, :], src(t))
            last.then_inc(n_st, 1)
            dve.wait_ge(n_st, at(m + 1))
            dve.sem_inc(q.apart, 1)
            for t in range(TPC):
                last = dve.bn_aggr(mv_[:, t, :], st_[:, t, :])
            last.then_inc(n_ag, 1)
            dve.wait_ge(n_sd, at(m + 1))
            dve.reciprocal(out_ln[:, :, 0:1], std_[:]).then_inc(n_rc, 1)
            dve.wait_ge(n_rc, at(m + 1))
            dve.scalar_tensor_tensor(out=out_ln[:, :, 1:2], in0=mv_[:, :, 0:1], scalar=-1.0, in1=out_ln[:, :, 0:1],
                                     op0=ALU.mult, op1=ALU.mult).then_inc(n_rd, 1)

        def std_of(act, m, mv_, std_, n_ag, n_sd):
            act.wait_ge(n_ag, at(m + 1))
            act.activation(std_[:], mv_[:, :, 1:2], ACT.Sqrt, bias=s.eps[:, 0:1]).then_inc(n_sd, 1)

        def normalize(act, dst, src, ln_, done):
            for t in range(TPC):
                last = act.activation(dst[:, t, :], src(t), ACT.Identity, scale=ln_(t, 0), bias=ln_(t, 1))
            last.then_inc(done, 1)

        def row(c, t):
            return ds(TPC * c + t, 1)

        def xs_tile(m):
            return lambda t: s.xs[:, row(m, t), :].rearrange("p a d -> p (a d)")

        def ln2_of(m):
            return lambda t, n: s.ln2[:, row(m, t), n:n + 1].rearrange("p a b -> p (a b)")

        def transpose_chunk(dst, src):
            for h in range(DK):
                for t in range(TPC):
                    last = nc.tensor.transpose(dst[h][:, t * P:(t + 1) * P], src[:, t, h * P:(h + 1) * P], s.ident[:])
            return last

        def pair_product(out_, w, wcols, xv, xcols, x_moves):
            steps = [(a, b, h) for h in range(DK) for a, b in ((0, 0), (0, 1), (1, 0))]
            for n, (a, b, h) in enumerate(steps):
                wa, xa_ = w[a][:, h, wcols], xv[b][:, h, xcols]
                last = nc.tensor.matmul(out_, wa if x_moves else xa_, xa_ if x_moves else wa,
                                        start=(n == 0), stop=(n == len(steps) - 1))
            return last

        def ring_wait(pe, c, i):
            if i >= 4:
                pe.wait_ge(q.combined, at(32 * c + 2 * (i - 3) if exists(c) else 32 * NCH))
                if not exists(c):
                    pe.wait_ge(q.qk_rest, at(4 * (c - 2) + (i - 16) + 1))
            else:
                pe.wait_ge(q.combined, at(32 * (c - 1) + 2 * (13 + i)))
                if first:
                    pe.wait_ge(q.qk_rest, at(4 * (c - 2) + i + 1))

        with nc.Block() as block:
            @block.sync
            def _(sp):
                for one in every:
                    sp.sem_inc(one, CREDIT)

                def load_attention(m, par):
                    cols = ds(CH * m, CH)
                    sp.wait_ge(q.att_ready, at(m - 1))
                    loaded = (q.num_loaded0, q.num_loaded1)[par]
                    sp.dma_start(num[par][:], s.att_num[:, cols].rearrange("(k p) n -> p k n", p=P)).then_inc(loaded, 16)
                    for h in range(DK):
                        rows = s.att_rec[h * KT:(h + 1) * KT, cols].unsqueeze(1).broadcast_to([KT, HD, CH])
                        sp.dma_start(rec[par][:, h, :], rows).then_inc(loaded, 16)

                def store_parts(m):
                    for j in range(4):
                        dst = (s.q_parts, s.k_parts)[j // 2]
                        sp.wait_ge(q.qk_lo, at(4 * m + j + 1))
                        sp.dma_start(dst[:, (j % 2) * P:(j % 2 + 1) * P, ds(CH * m, CH)].rearrange("a p n -> p a n"),
                                     part[j][:]).then_inc(q.stored[j], 16)

                def slot(c, par, nth):
                    if first:
                        if exists(c - 1):
                            store_parts(c - 1)
                    else:
                        if exists(c + 3):
                            load_attention(c + 3, 1 - par)
                        sp.wait_ge(q.x_ready, at(TPC * c + TPC))
                        sp.dma_start(s.out[:, tiles(c), :], s.xs[:, tiles(c), :]).then_inc(q.written, 16)

                if not first:
                    load_attention(0, 0)
                    load_attention(1, 1)
                    load_attention(2, 0)
                slots(sp, slot)
                if first:
                    for j in range(4):
                        sp.wait_ge(q.stored[j], at(16 * NCH))
                else:
                    sp.wait_ge(q.written, at(16 * NCH))

            @block.gpsimd
            def _(pool):
                for par in range(2):
                    pool.memset(mask[par][:], 0.0).then_inc(q.mask_zero, 1)

                def add_tiles(c, which):
                    for t in which:
                        pool.wait_ge(q.combined, at(8 * (TPC * c + t) + 8))
                        pool.sem_inc(q.apart, 1)
                        pool.tensor_tensor(s.xs[:, row(c, t), :].rearrange("p a d -> p (a d)"), acc[t % 2][0][:],
                                           acc[t % 2][1][:], ALU.add).then_inc(q.x_ready, 1)

                def low_parts(m):
                    for j in range(4):
                        pool.wait_ge(q.qk_mid, at(4 * m + j + 1))
                        pool.tensor_tensor(part[j][:, 2, :], rest[j % 2][:], part[j][:, 1, :],
                                           ALU.subtract).then_inc(q.qk_lo, 1)

                def add_bias(m):
                    pool.wait_ge(q.resid_ready, at(m + 1))
                    pool.wait_ge(q.xa_ready, at(2 * m))
                    wide = s.bproj[:].unsqueeze(1).broadcast_to([P, TPC, D])
                    pool.tensor_tensor(residb[:], resid[:], wide, ALU.add).then_inc(q.resid_bias, 1)

                def shift_x(m):
                    pool.wait_ge(q.x2_ready, at(m))
                    pool.sem_inc(q.apart, 1)
                    pool.tensor_tensor(xb[:], s.xs[:, tiles(m), :], s.beta[:].unsqueeze(1).broadcast_to([P, TPC, D]),
                                       ALU.add).then_inc(q.x_shifted, 1)

                def affine_add(m):
                    pool.wait_ge(q.y_ready, at(m + 1))
                    pool.tensor_tensor(yg[:], yn[:], s.gamma[:].unsqueeze(1).broadcast_to([P, TPC, D]),
                                       ALU.mult).then_inc(q.scaled, 1)
                    pool.wait_ge(q.scaled, at(m + 1))
                    pool.wait_ge(q.x_shifted, at(m + 1))
                    pool.sem_inc(q.apart, 1)
                    pool.tensor_tensor(s.xs[:, tiles(m), :], yg[:], xb[:], ALU.add).then_inc(q.x2_ready, 1)

                def slot(c, par, nth):
                    if first:
                        if exists(c):
                            add_tiles(c, range(TPC))
                        if exists(c - 1):
                            low_parts(c - 1)
                    else:
                        if exists(c + 2):
                            shift_x(c + 2)
                            affine_add(c + 2)
                        add_tiles(c, (0, 1))
                        if exists(c + 3):
                            add_bias(c + 3)
                        add_tiles(c, (2, 3))

                if not first:
                    for m in range(2):
                        add_bias(m)
                        shift_x(m)
                        affine_add(m)
                    add_bias(2)
                slots(pool, slot)

            @block.scalar
            def _(act):
                def split_hi(m, par):
                    act.wait_ge(q.turned, at(m + 1))
                    act.wait_ge(q.ffn_bank, at(16 * (m - 1)))
                    for h in range(DK):
                        act.activation(xt[par][0][:, h, :], pt[h][:], ACT.Copy).then_inc(q.hi_ready, 1)

                def logits_out(m):
                    act.wait_ge(q.router_done, at(m + 1))
                    act.wait_ge(q.logits_turned, at(m))
                    act.activation(logits_t[:], pr[0:NE, :], ACT.Identity, bias=s.brouter[:, 0:1]).then_inc(q.logits_ready, 1)

                def mask_out(m, par):
                    act.wait_ge(q.mask_turned, at(m + 1))
                    act.wait_ge(q.bias_done, at(2 * (m - 1)))
                    act.activation(mask_t[par][:], pr_b[:], ACT.Copy).then_inc(q.maskt_ready, 1)

                def bias_out(c, pair):
                    act.wait_ge(q.bias_done, at(2 * c + pair + 1))
                    act.wait_ge(q.combined, at(8 * (TPC * (c - 1) + 2 * pair + 2)))
                    act.activation(ybias[pair][:].rearrange("p t d -> p (t d)"), pb[:], ACT.Copy).then_inc(q.bias_ready, 1)

                def norm(m):
                    std_of(act, m, mv, std, q.normed_aggr, q.std_done)
                    act.wait_ge(q.norm_ready, at(m + 1))
                    act.wait_ge(q.turned, at(m))
                    act.sem_inc(q.apart, 1)
                    normalize(act, xh, xs_tile(m), lambda t, n: ln[:, t, n:n + 1], q.xh_ready)

                def norm2(m):
                    std_of(act, m, mv2, std2, q.aggr2, q.std2)
                    act.wait_ge(q.norm2, at(m + 1))
                    act.wait_ge(q.turned2, at(m))
                    act.sem_inc(q.apart, 1)
                    normalize(act, xh2, xs_tile(m), ln2_of(m), q.xh2_ready)

                def split2(m):
                    act.wait_ge(q.turned2, at(m + 1))
                    act.wait_ge(q.v_bank, at(2 * m))
                    act.wait_ge(q.qk_bank, at(4 * m))
                    act.wait_ge(q.lo2_ready, at(m))
                    for h in range(DK):
                        act.activation(xt2[:, h, :], pt[h][:], ACT.Copy)
                        last = act.activation(xt2r[0][:, h, :], pt[h][:], ACT.Copy)
                    last.then_inc(q.hi2_ready, 1)

                def v_out(m):
                    for pair in range(2):
                        act.wait_ge(q.v_bank, at(2 * m + pair + 1))
                        act.sem_inc(q.apart, 1)
                        act.activation(s.v_all[:, ds(TPC * m + 2 * pair, 2), :], pt[pair][:].rearrange("p (t d) -> p t d", d=D),
                                       ACT.Copy).then_inc(q.v_ready, 1)

                def qk_hi(m, j):
                    act.wait_ge(q.qk_bank, at(4 * m + j + 1))
                    act.wait_ge(q.stored[j], at(16 * m))
                    act.activation(part[j][:, 0, :], ring[j][:], ACT.Copy).then_inc(q.qk_hi, 1)

                def qk_mid(m, j):
                    act.wait_ge(q.qk_rest, at(4 * m + j + 1))
                    act.activation(part[j][:, 1, :], rest[j % 2][:], ACT.Copy).then_inc(q.qk_mid, 1)

                def residual(m):
                    act.wait_ge(q.resid_bias, at(m))
                    act.sem_inc(q.apart, 1)
                    normalize(act, resid, xs_tile(m), ln2_of(m), q.resid_ready)

                def norm3(m):
                    std_of(act, m, mv3, std3, q.aggr3, q.std3)
                    act.wait_ge(q.norm3, at(m + 1))
                    act.wait_ge(q.scaled, at(m))
                    normalize(act, yn, lambda t: xa[:, t, :], lambda t, n: ln3[:, t, n:n + 1], q.y_ready)

                def slot(c, par, nth):
                    if exists(c):
                        bias_out(c, 0)
                    if first and exists(c - 1):
                        norm2(c - 1)
                    if not first and exists(c + 2):
                        norm3(c + 2)
                    if exists(c + 1):
                        split_hi(c + 1, 1 - par)
                        logits_out(c + 1)
                    if exists(c):
                        bias_out(c, 1)
                    if first and exists(c - 1):
                        split2(c - 1)
                        v_out(c - 1)
                    if not first and exists(c + 3):
                        residual(c + 3)
                    if exists(c + 2):
                        norm(c + 2)
                    if exists(c + 1):
                        mask_out(c + 1, 1 - par)
                    if first and exists(c - 1):
                        for j in (0, 2):
                            qk_hi(c - 1, j)
                            qk_hi(c - 1, j + 1)
                            qk_mid(c - 1, j)
                            qk_mid(c - 1, j + 1)

                if not first:
                    residual(0)
                    residual(1)
                    norm3(0)
                norm(0)
                split_hi(0, 0)
                if not first:
                    norm3(1)
                logits_out(0)
                norm(1)
                mask_out(0, 0)
                if not first:
                    residual(2)
                slots(act, slot)

            @block.tensor
            def _(pe):
                def turn(m):
                    pe.wait_ge(q.xh_ready, at(m + 1))
                    if first:
                        pe.wait_ge(q.v_ready, at(2 * (m - 2)))
                    elif isinstance(m, int):
                        pe.wait_ge(q.xa_ready, at(2 * min(m + 2, NCH) if m else 2))
                    else:
                        pe.wait_ge(q.xa_ready, at(2 * (m + 2)))
                    pe.wait_ge(q.lo_ready, at(2 * m))
                    transpose_chunk(pt, xh).then_inc(q.turned, 1)

                def router(m, par):
                    pe.wait_ge(q.lo_ready, at(2 * m + 2))
                    pe.wait_ge(q.maskt_ready, at(m))
                    pair_product(pr[0:NE, :], s.wr, slice(0, NE), xt[par], slice(0, CH), True).then_inc(q.router_done, 1)

                def turn_logits(m):
                    pe.wait_ge(q.logits_ready, at(m + 1))
                    pe.sem_inc(q.apart, 1)
                    for t in range(TPC):
                        last = nc.tensor.transpose(pr[:, t * NE:(t + 1) * NE], logits_t[:, t * P:(t + 1) * P],
                                                   s.ident[0:NE, 0:NE])
                    last.then_inc(q.logits_turned, 1)

                def turn_mask(m, par):
                    pe.wait_ge(q.mask_ready, at(m + 1))
                    nc.tensor.transpose(pr_b[:], mask[par][:].rearrange("p t e -> p (t e)"),
                                        s.ident_b[:]).then_inc(q.mask_turned, 1)

                def bias(c, par, pair):
                    pe.wait_ge(q.maskt_ready, at(c + 1))
                    pe.wait_ge(q.bias_ready, at(2 * c + pair))
                    for i in range(2):
                        last = nc.tensor.matmul(pb[:, i * D:(i + 1) * D], mask_t[par][:], s.bias_rows[:, 2 * pair + i, :],
                                                start=True, stop=True)
                    last.then_inc(q.bias_done, 1)

                def experts(c, par, t):
                    for n in range(4):
                        ring_wait(pe, c, 4 * t + n)
                        pair_product(ring[n][:], s.we, slice(n * CH, (n + 1) * CH), xt[par], slice(t * P, (t + 1) * P),
                                     False).then_inc(q.ffn_bank, 1)

                def turn2(m):
                    pe.wait_ge(q.xh2_ready, at(m + 1))
                    pe.wait_ge(q.lo_ready, at(2 * min(m + 3, NCH) if isinstance(m, int) else 2 * (m + 3)))
                    pe.wait_ge(q.v_ready, at(2 * m))
                    transpose_chunk(pt, xh2).then_inc(q.turned2, 1)

                def values(m):
                    pe.wait_ge(q.hi2_ready, at(m + 1))
                    for pair in range(2):
                        for i in range(2):
                            for h in range(DK):
                                t = 2 * pair + i
                                last = nc.tensor.matmul(pt[pair][:, i * D:(i + 1) * D], xt2[:, h, t * P:(t + 1) * P],
                                                        s.wv[:, h, :], start=(h == 0), stop=(h == DK - 1))
                        last.then_inc(q.v_bank, 1)

                def queries_keys(m, c):
                    pe.wait_ge(q.lo2_ready, at(m + 1))
                    for j in range(4):
                        ring_wait(pe, c, 16 + j)
                        pair_product(ring[j][:], s.wqk, slice(j * P, (j + 1) * P), xt2r, slice(0, CH),
                                     True).then_inc(q.qk_bank, 1)

                def project(m, par):
                    pe.wait_ge(q.att_ready, at(m + 1))
                    pe.wait_ge(q.lo_ready, at(2 if isinstance(m, int) and m == 1 else 2 * (m - 1)))
                    pe.wait_ge(q.xa_ready, at(2 * m))
                    for pair in range(2):
                        for i in range(2):
                            for h in range(DK):
                                t = 2 * pair + i
                                last = nc.tensor.matmul(pt[pair][:, i * D:(i + 1) * D], att[par][:, h, t * P:(t + 1) * P],
                                                        s.wp[:, h, :], start=(h == 0), stop=(h == DK - 1))
                        last.then_inc(q.proj_bank, 1)

                def slot(c, par, nth):
                    if not first and exists(c + 2):
                        project(c + 2, par)
                    if exists(c):
                        bias(c, par, 0)
                        experts(c, par, 0)
                    if exists(c + 1):
                        turn(c + 1)
                    if exists(c):
                        experts(c, par, 1)
                    if exists(c + 1):
                        router(c + 1, 1 - par)
                    if first and exists(c - 1):
                        turn2(c - 1)
                    if exists(c):
                        bias(c, par, 1)
                        experts(c, par, 2)
                    if exists(c + 1):
                        turn_logits(c + 1)
                    if first and exists(c - 1):
                        values(c - 1)
                    if exists(c):
                        experts(c, par, 3)
                    if exists(c + 1):
                        turn_mask(c + 1, 1 - par)
                    if first and exists(c - 1):
                        queries_keys(c - 1, c)

                if not first:
                    project(0, 0)
                turn(0)
                if not first:
                    project(1, 1)
                router(0, 0)
                turn_logits(0)
                turn_mask(0, 0)
                slots(pe, slot)

            @block.vector
            def _(dve):
                def norm(m):
                    if not first:
                        dve.wait_ge(q.x2_ready, at(m + 1))
                        dve.sem_inc(q.apart, 1)
                    norm_stats(dve, xs_tile(m), m, st, mv, std, ln, q.normed_stats, q.normed_aggr, q.std_done,
                               q.rstd_done, q.norm_ready)

                def norm2(m):
                    dve.wait_ge(q.x_ready, at(TPC * m + TPC))
                    dve.sem_inc(q.apart, 1)
                    norm_stats(dve, xs_tile(m), m, st2, mv2, std2, s.ln2[:, tiles(m), :], q.st2, q.aggr2, q.std2,
                               q.rstd2, q.norm2)

                def split_lo(m, par):
                    for h in range(DK):
                        dve.wait_ge(q.hi_ready, at(2 * m + h + 1))
                        dve.tensor_tensor(xt[par][1][:, h, :], pt[h][:], xt[par][0][:, h, :].bitcast(F32),
                                          ALU.subtract).then_inc(q.lo_ready, 1)

                def split2(m):
                    dve.wait_ge(q.hi2_ready, at(m + 1))
                    dve.wait_ge(q.qk_bank, at(4 * m))
                    dve.tensor_tensor(xt2r[1][:], xt2[:], xt2r[0][:].bitcast(F32), ALU.subtract).then_inc(q.lo2_ready, 1)

                def ranks(m, par):
                    dve.wait_ge(q.logits_turned, at(m + 1))
                    dve.tensor_copy(logits[:], pr[:, 0:TPC * NE]).then_inc(q.logits_copied, 1)
                    dve.wait_ge(q.logits_copied, at(m + 1))
                    other = logits[:].rearrange("p (t e) -> p t e", e=NE).unsqueeze(2).broadcast_to([P, TPC, NE, NE])
                    own = logits[:].unsqueeze(2).broadcast_to([P, TPC * NE, NE])
                    wide = lambda a: a[:].rearrange("p (t e) f -> p t e f", e=NE)
                    own4 = own.rearrange("p (t e) f -> p t e f", e=NE)
                    dve.tensor_tensor(wide(eq), other, own4, ALU.is_equal).then_inc(q.rank_step, 1)
                    dve.tensor_tensor(wide(gt), other, own4, ALU.is_gt).then_inc(q.rank_step, 1)
                    dve.wait_ge(q.rank_step, at(5 * m + 1))
                    dve.tensor_tensor(wins[:], eq[:], s.before[:], ALU.mult).then_inc(q.rank_step, 1)
                    dve.wait_ge(q.rank_step, at(5 * m + 3))
                    dve.tensor_tensor(eq[:], wins[:], gt[:], ALU.add).then_inc(q.rank_step, 1)
                    dve.wait_ge(q.rank_step, at(5 * m + 4))
                    dve.tensor_reduce(rank[:], eq[:], AX.X, ALU.add).then_inc(q.rank_step, 1)
                    dve.wait_ge(q.rank_step, at(5 * m + 5))
                    dve.wait_ge(q.mask_zero, at(2))
                    dve.wait_ge(q.mask_turned, at(m - 1))
                    copies = rank[:].rearrange("p (t e) -> p t e", e=NE).unsqueeze(2).broadcast_to([P, TPC, 3, NE])
                    dve.tensor_scalar(mask[par][:, :, 0:3 * NE].rearrange("p t (a e) -> p t a e", e=NE), copies,
                                      2.0, 0.5, ALU.is_lt, ALU.mult).then_inc(q.mask_ready, 1)

                def combine(c, par, t):
                    done = 8 * (TPC * c + t)
                    for n in range(4):
                        dve.wait_ge(q.ffn_bank, at(16 * c + 4 * t + n + 1))
                        if n == 0:
                            dve.wait_ge(q.bias_ready, at(2 * c + t // 2 + 1))
                            dve.wait_ge(q.mask_ready, at(c + 1))
                            dve.wait_ge(q.x_ready, at(TPC * c + t - 1))
                        for i in range(2):
                            a = acc[t % 2][i]
                            if n:
                                dve.wait_ge(q.combined, at(done + 2 * (n - 1) + i + 1))
                                base = a[:]
                            else:
                                base = (ybias[t // 2][:, t % 2, :], xs_tile(c)(t))[i]
                            dve.scalar_tensor_tensor(out=a[:], in0=ring[n][:, i * D:(i + 1) * D],
                                                     scalar=mask[par][:, t, 2 * n + i:2 * n + i + 1], in1=base,
                                                     op0=ALU.mult, op1=ALU.add).then_inc(q.combined, 1)

                def qk_rests(m):
                    for j in range(4):
                        dve.wait_ge(q.qk_hi, at(4 * m + j + 1))
                        dve.wait_ge(q.qk_lo, at(4 * m + j - 1))
                        dve.tensor_tensor(rest[j % 2][:], ring[j][:], part[j][:, 0, :], ALU.subtract).then_inc(q.qk_rest, 1)

                def attended(m, par, nth):
                    dve.wait_ge((q.num_loaded0, q.num_loaded1)[par], at(16 * 3 * (nth + 1)))
                    dve.wait_ge(q.proj_bank, at(2 * (m - 1)))
                    dve.tensor_tensor(att[par][:], num[par][:], rec[par][:], ALU.mult).then_inc(q.att_ready, 1)

                def add_residual(m):
                    dve.wait_ge(q.resid_bias, at(m + 1))
                    dve.wait_ge(q.y_ready, at(m))
                    for pair in range(2):
                        dve.wait_ge(q.proj_bank, at(2 * m + pair + 1))
                        dve.tensor_tensor(xa[:, 2 * pair:2 * pair + 2, :], pt[pair][:].rearrange("p (t d) -> p t d", d=D),
                                          residb[:, 2 * pair:2 * pair + 2, :], ALU.add).then_inc(q.xa_ready, 1)
                    dve.wait_ge(q.xa_ready, at(2 * m + 2))
                    norm_stats(dve, lambda t: xa[:, t, :], m, st3, mv3, std3, ln3, q.st3, q.aggr3, q.std3, q.rstd3, q.norm3)

                def slot(c, par, nth):
                    if first and exists(c - 1):
                        norm2(c - 1)
                    if not first and exists(c + 2):
                        add_residual(c + 2)
                    if exists(c):
                        combine(c, par, 0)
                    if exists(c + 1):
                        split_lo(c + 1, 1 - par)
                    if exists(c):
                        combine(c, par, 1)
                        combine(c, par, 2)
                    if exists(c + 1):
                        ranks(c + 1, 1 - par)
                    if first and exists(c - 1):
                        split2(c - 1)
                    if exists(c + 2):
                        norm(c + 2)
                    if exists(c):
                        combine(c, par, 3)
                    if not first and exists(c + 3):
                        attended(c + 3, 1 - par, nth + 1 + par)
                    if first and exists(c - 1):
                        qk_rests(c - 1)

                if not first:
                    attended(0, 0, 0)
                    add_residual(0)
                norm(0)
                if not first:
                    attended(1, 1, 0)
                split_lo(0, 0)
                if not first:
                    add_residual(1)
                ranks(0, 0)
                norm(1)
                if not first:
                    attended(2, 0, 1)
                slots(dve, slot)


def query_blocks():
    for i in range(KT):
        for lo in range(0, (i + 1) * P, CH):
            width = min(CH, (i + 1) * P - lo)
            yield i, lo, width, CH // width, lo + width == (i + 1) * P


def key_blocks():
    for half in range(SEQ // CH):
        for j in range((half + 1) * CH // P):
            start = max(0, j * P - half * CH)
            yield j, half, start, CH - start


def max_units():
    return [(i, lo, width, range(c, c + hp), diagonal) for i, lo, width, hp, diagonal in query_blocks()
            for c in range(0, GH, hp)]


def exp_units():
    return [[range(c, c + CH // width) for c in range(0, GH, CH // width)] for _, _, _, width in key_blocks()]


def attention_phase(nc, s):
    keys = list(key_blocks())
    eunits = exp_units()
    munits = max_units()
    nexp = sum(len(u) for u in eunits)
    nmax = len(munits) + 1
    early = 9
    nkb = len(keys)
    assert nmax % 3 == 0
    with ExitStack() as ctx:
        def sb(name, shape, dt=F32):
            return ctx.enter_context(nc.sbuf_tensor(f"b_{name}", shape, dt))

        every = []

        def sem(name):
            every.append(ctx.enter_context(nc.semaphore(f"b_{name}")))
            return every[-1]

        qs = [sb(f"qs{u}", [MROWS, GH, SEQ], BF16) for u in range(3)]
        ks = [sb(f"ks{u}", [MROWS, GH, SEQ], BF16) for u in range(3)]
        vs = [sb(f"vs{u}", [P, KT, GH, SLOT]) for u in range(3)]
        probs = [sb(f"probs{n}", [P, GH, CH]) for n in range(3)]
        oev = [sb(f"oev{u}", [P, SEQ]) for u in range(3)]
        den = [sb(f"den{u}", [P, SEQ // SLOT]) for u in range(3)]
        rcp = [sb(f"rcp{u}", [P, SEQ // SLOT]) for u in range(3)]
        neg1 = [sb(f"neg1{u}", [P, GH, KT]) for u in range(3)]
        neg2 = [sb(f"neg2{u}", [P, GH, KT - CH // P]) for u in range(3)]
        turned = sb("turned", [GH * KT, P])
        turned_rest = sb("turned_rest", [GH * KT, P])
        mparts = [sb(f"mparts{u}", [GH * KT, 3, P], BF16) for u in range(3)]
        masked_b = sb("masked_b", [P, P], BF16)
        es = [ctx.enter_context(nc.psum_tensor(f"b_es{n}", [P, CH], F32)) for n in range(3)]
        ms = [ctx.enter_context(nc.psum_tensor(f"b_ms{n}", [P, CH], F32)) for n in range(3)]
        os_ = [ctx.enter_context(nc.psum_tensor(f"b_os{n}", [P, CH], F32)) for n in range(2)]

        consts, vones = sem("consts"), sem("vones")
        loaded = [sem(f"loaded{u}") for u in range(3)]
        mplaced = [sem(f"mplaced{u}") for u in range(3)]
        stored = [sem(f"stored{u}") for u in range(3)]
        den_placed = [sem(f"den_placed{u}") for u in range(3)]
        mscore, mread = sem("mscore"), sem("mread")
        mfinal, mpart = sem("mfinal"), sem("mpart")
        escore, expd, kept, summed = sem("escore"), sem("expd"), sem("kept"), sem("summed")
        apart = sem("apart")
        rec_stored = [sem(f"rec_stored{u}") for u in range(3)]
        v_copied, o_copied, inverted = sem("v_copied"), sem("o_copied"), sem("inverted")

        def slots(engine, slot):
            slot(Group(0, 0))
            with engine.Fori(0, (NG - 4) // 3) as i:
                for u in range(1, 4):
                    slot(Group(i, 0) + u)
            for g in range(NG - 3, NG):
                slot(Group(0, 0) + g)

        def exists(g):
            return not isinstance(g.n, int) or 0 <= g.n < NG

        def stream(g):
            rest = [(g + 1, n) for n in range(early, len(munits))] if exists(g + 1) else []
            new = [(g + 2, n) for n in range(early)] if exists(g + 2) else []
            turn = [(g + 1, None)] if exists(g + 1) else []
            return rest + new[:3] + turn + new[3:]

        first_stream = ([(Group(0, 0), n) for n in range(len(munits))] + [(Group(0, 1), n) for n in range(3)] + [(Group(0, 0), None)]
                        + [(Group(0, 1), n) for n in range(3, early)])

        def place(g, n):
            return nmax + early + nmax * g.n + n, (early + n) % 3

        def exp_bank(g, unit):
            return (nexp * g.u + unit) % 3

        unit0 = [sum(len(u) for u in eunits[:b]) for b in range(nkb + 1)]
        sel_blocks = [b for b, (j, half, start, width) in enumerate(keys) if half * CH + start == j * P]

        with nc.Block() as block:
            @block.sync
            def _(sp):
                for one in every:
                    sp.sem_inc(one, CREDIT)

                def load(g):
                    sp.wait_ge(escore, at(nexp * (g.n - 2)))
                    head, tok = (g.n % HGS) * (GH * HD), (g.n // HGS) * SEQ
                    for part, (piece, reps) in enumerate(PARTS):
                        rows = slice(piece * HD, (piece + reps) * HD)
                        q_src = s.q_parts[part, ds(head, GH * HD), ds(tok, SEQ)].rearrange("(c r) n -> r c n", r=HD)
                        for a in range(reps):
                            sp.dma_start(qs[g.u][(piece + a) * HD:(piece + a + 1) * HD, :, :], q_src).then_inc(loaded[g.u], 16)
                            k_src = s.k_parts[a, ds(head, GH * HD), ds(tok, SEQ)].rearrange("(c r) n -> r c n", r=HD)
                            sp.dma_start(ks[g.u][(piece + a) * HD:(piece + a + 1) * HD, :, :], k_src).then_inc(loaded[g.u], 16)

                def place_maxima(g):
                    sp.wait_ge(mpart, at(5 * g.n + 5))
                    for part in range(3):
                        sp.dma_start(qs[g.u][ROWS + part:ROWS + part + 1, :, :].rearrange("a c n -> a (c n)"),
                                     mparts[g.u][:, part, :]).then_inc(mplaced[g.u], 16)

                def store(g):
                    head, tok = (g.n % HGS) * (GH * HD), (g.n // HGS) * SEQ
                    sp.wait_ge(o_copied, at(2 * g.n + 2))
                    for c in range(GH):
                        sp.dma_start(s.att_num[ds(head + c * HD, HD), ds(tok, SEQ)],
                                     oev[g.u][SLOT * c:SLOT * c + HD, :]).then_inc(stored[g.u], 16)
                        sp.dma_start(den[g.u][SLOT * c:SLOT * (c + 1), :],
                                     oev[g.u][SLOT * c + HD:SLOT * c + HD + 1, :]).then_inc(den_placed[g.u], 16)

                def store_inverse(g):
                    tok = (g.n // HGS) * SEQ
                    sp.wait_ge(inverted, at(g.n + 1))
                    for c in range(GH):
                        dst = s.att_rec[ds((g.n % HGS) * GH + c, 1), ds(tok, SEQ)].rearrange("a (p n) -> (a p) n", p=SLOT)
                        sp.dma_start(dst, rcp[g.u][SLOT * c:SLOT * (c + 1), :]).then_inc(rec_stored[g.u], 16)

                load(Group(0, 0))
                load(Group(0, 1))
                place_maxima(Group(0, 0))

                def slot(g):
                    if exists(g + 2):
                        load(g + 2)
                    if exists(g + (-1)):
                        store(g + (-1))
                        store_inverse(g + (-1))
                    if exists(g + 1):
                        place_maxima(g + 1)

                slots(sp, slot)
                store(Group(0, 0) + (NG - 1))
                store_inverse(Group(0, 0) + (NG - 1))
                for u in range(3):
                    sp.wait_ge(stored[u], at(16 * GH * len(range(u, NG, 3))))
                    sp.wait_ge(rec_stored[u], at(16 * GH * len(range(u, NG, 3))))

            @block.gpsimd
            def _(pool):
                def copy_values(g):
                    src = s.v_all[:, ds((g.n // HGS) * KT, KT), ds((g.n % HGS) * (GH * HD), GH * HD)]
                    pool.tensor_copy(vs[g.u][:, :, :, 0:HD], src.rearrange("p j (c r) -> p j c r", r=HD)).then_inc(v_copied, 1)

                pool.memset(masked_b[:], 0.0).then_inc(consts, 1)
                pool.wait_ge(consts, at(1))
                pool.affine_select(out=masked_b[:], in_=masked_b[:], compare_op=ALU.is_ge, fill=MASKED, base=0,
                                   pattern=[[-1, P]], channel_multiplier=1).then_inc(consts, 1)
                pool.wait_ge(consts, at(2))
                for u in range(3):
                    pool.memset(vs[u][:, :, :, HD:SLOT], 1.0).then_inc(vones, 1)
                    pool.wait_ge(vones, at(2 * u + 1))
                    pool.memset(ks[u][ROWS:MROWS, :, :], 1.0).then_inc(vones, 1)
                    pool.wait_ge(vones, at(2 * u + 2))
                copy_values(Group(0, 0))

                def slot(g):
                    for b, (j, half, start, width) in enumerate(keys):
                        if b in sel_blocks:
                            pool.wait_ge(expd, at(nexp * g.n + unit0[b + 1]))
                            pool.sem_inc(apart, 1)
                            part = probs[b % 3][:, :, 0:P]
                            pool.affine_select(out=part, in_=part, compare_op=ALU.is_ge, fill=0.0, base=0,
                                               pattern=[[0, GH], [1, P]], channel_multiplier=-1).then_inc(kept, 1)
                        if b == 4 and exists(g + 1):
                            pool.wait_ge(summed, at(nkb * (g.n - 1)))
                            copy_values(g + 1)

                slots(pool, slot)

            @block.scalar
            def _(act):
                def copy_out(g, half):
                    act.wait_ge(summed, at(nkb * g.n + (4 if half == 0 else nkb)))
                    if isinstance(g.turn, int) and g.turn == 0:
                        pass
                    else:
                        act.wait_ge(stored[g.u], at(16 * GH * g.turn))
                        act.wait_ge(den_placed[g.u], at(16 * GH * g.turn))
                    act.activation(oev[g.u][:, half * CH:(half + 1) * CH], os_[half][:], ACT.Copy).then_inc(o_copied, 1)

                def slot(g):
                    for b, (j, half, start, width) in enumerate(keys):
                        for n, heads in enumerate(eunits[b]):
                            unit = unit0[b] + n
                            act.wait_ge(escore, at(nexp * g.n + unit + 1))
                            if n == 0:
                                act.wait_ge(summed, at(nkb * g.n + b - 2))
                            hp = len(heads)
                            act.activation(probs[b % 3][:, heads[0]:heads[0] + hp, 0:width],
                                           es[exp_bank(g, unit)][:, 0:hp * width].rearrange("p (h w) -> p h w", w=width),
                                           ACT.Exp, scale=SCALE).then_inc(expd, 1)
                        if b == 1 and exists(g + (-1)):
                            copy_out(g + (-1), 1)
                        if b == 5:
                            copy_out(g, 0)

                slots(act, slot)
                copy_out(Group(0, 0) + (NG - 1), 1)

            @block.tensor
            def _(pe):
                def max_entry(entry, position, bank):
                    g, n = entry
                    pe.wait_ge(mread, at(position - 2))
                    if n is None:
                        pe.wait_ge(mfinal, at(g.n + 1))
                        nc.tensor.transpose(ms[bank][0:GH * KT, 0:P], neg1[g.u][:].rearrange("p c i -> p (c i)"),
                                            s.ident[:]).then_inc(mscore, 1)
                        return
                    if n == 0:
                        pe.wait_ge(loaded[g.u], at(16 * 12 * (g.turn + 1)))
                    i, lo, width, heads, diagonal = munits[n]
                    for a, c in enumerate(heads):
                        last = nc.tensor.matmul(ms[bank][:, a * width:(a + 1) * width], qs[g.u][0:ROWS, c, i * P:(i + 1) * P],
                                                ks[g.u][0:ROWS, c, lo:lo + width], start=True, stop=not diagonal)
                        if diagonal:
                            last = nc.tensor.matmul(ms[bank][:, (a + 1) * width - P:(a + 1) * width], s.ident_b[:],
                                                    masked_b[:], start=False, stop=True)
                    last.then_inc(mscore, 1)

                def exp_unit(g, b, n):
                    j, half, start, width = keys[b]
                    unit = unit0[b] + n
                    if unit == 0:
                        pe.wait_ge(mplaced[g.u], at(16 * 3 * (g.turn + 1)))
                    pe.wait_ge(expd, at(nexp * g.n + unit - 2))
                    for a, c in enumerate(eunits[b][n]):
                        first_q = half * CH + start
                        last = nc.tensor.matmul(es[exp_bank(g, unit)][:, a * width:(a + 1) * width],
                                                ks[g.u][:, c, j * P:(j + 1) * P], qs[g.u][:, c, first_q:first_q + width],
                                                start=True, stop=True)
                    last.then_inc(escore, 1)

                def products(g, b):
                    j, half, start, width = keys[b]
                    pe.wait_ge(expd, at(nexp * g.n + unit0[b + 1]))
                    if b in sel_blocks:
                        pe.wait_ge(kept, at(len(sel_blocks) * g.n + sel_blocks.index(b) + 1))
                    if b == 0:
                        pe.wait_ge(v_copied, at(g.n + 1))
                    if j == 0:
                        pe.wait_ge(o_copied, at(2 * g.n - 1 + half))
                    for c in range(GH):
                        last = nc.tensor.matmul(os_[half][SLOT * c:SLOT * (c + 1), start:CH], vs[g.u][:, j, c, :],
                                                probs[b % 3][:, c, 0:width], start=(j == 0),
                                                stop=(j == (half + 1) * CH // P - 1))
                    last.then_inc(summed, 1)

                pe.wait_ge(consts, at(2))
                pe.wait_ge(vones, at(6))
                for position, entry in enumerate(first_stream):
                    max_entry(entry, position, position % 3)

                def slot(g):
                    entries = list(enumerate(stream(g)))
                    tail = 5
                    per = max(0, len(entries) - tail) / nexp
                    for b in range(nkb):
                        for n in range(len(eunits[b])):
                            exp_unit(g, b, n)
                            due = len(stream(g)) - tail - int(per * (nexp - unit0[b] - n - 1))
                            while entries and entries[0][0] < due:
                                at, entry = entries.pop(0)
                                max_entry(entry, *place(g, at))
                        if b == 0 and exists(g + (-1)):
                            products(g + (-1), nkb - 1)
                        if b > 0:
                            products(g, b - 1)
                    for at, entry in entries:
                        max_entry(entry, *place(g, at))

                slots(pe, slot)
                products(Group(0, 0) + (NG - 1), nkb - 1)

            @block.vector
            def _(dve):
                def max_entry(entry, position, bank):
                    g, n = entry
                    dve.wait_ge(mscore, at(position + 1))
                    if n is None:
                        t, r, m = turned, turned_rest, mparts[g.u]
                        dve.tensor_copy(t[:], ms[bank][0:GH * KT, 0:P]).then_inc(mread, 1)
                        dve.wait_ge(mread, at(position + 1))
                        if not (isinstance(g.turn, int) and g.turn == 0):
                            dve.wait_ge(mplaced[g.u], at(16 * 3 * g.turn))
                        dve.tensor_copy(m[:, 0, :], t[:]).then_inc(mpart, 1)
                        dve.wait_ge(mpart, at(5 * g.n + 1))
                        dve.tensor_tensor(r[:], t[:], m[:, 0, :], ALU.subtract).then_inc(mpart, 1)
                        dve.wait_ge(mpart, at(5 * g.n + 2))
                        dve.tensor_copy(m[:, 1, :], r[:]).then_inc(mpart, 1)
                        dve.wait_ge(mpart, at(5 * g.n + 3))
                        dve.tensor_tensor(m[:, 2, :], r[:], m[:, 1, :], ALU.subtract).then_inc(mpart, 2)
                        return
                    i, lo, width, heads, diagonal = munits[n]
                    dst = neg1[g.u][:, heads[0]:heads[0] + len(heads), i:i + 1] if lo == 0 else \
                        neg2[g.u][:, heads[0]:heads[0] + len(heads), i - CH // P:i - CH // P + 1]
                    dve.tensor_reduce(dst, ms[bank][:, 0:len(heads) * width].rearrange("p (h w) -> p h w", w=width), AX.X,
                                      ALU.max, negate=True).then_inc(mread, 1)
                    if n == len(munits) - 1:
                        dve.wait_ge(mread, at(position + 1))
                        late = neg1[g.u][:, :, CH // P:KT]
                        dve.tensor_tensor(late, late, neg2[g.u][:], ALU.min).then_inc(mfinal, 1)

                for position, entry in enumerate(first_stream):
                    max_entry(entry, position, position % 3)

                def invert(g):
                    dve.wait_ge(den_placed[g.u], at(16 * GH * (g.turn + 1)))
                    dve.wait_ge(rec_stored[g.u], at(16 * GH * g.turn))
                    dve.reciprocal(rcp[g.u][:], den[g.u][:]).then_inc(inverted, 1)

                def slot(g):
                    for at, entry in enumerate(stream(g)):
                        max_entry(entry, *place(g, at))
                        if at == 16 and exists(g + (-1)):
                            invert(g + (-1))
                    if not stream(g) and exists(g + (-1)):
                        invert(g + (-1))

                slots(dve, slot)
                invert(Group(0, 0) + (NG - 1))


INPUTS = ("L0_attn_target", "L0_attn_w_qkv", "L0_attn_w_proj", "L0_attn_b_proj", "L0_attn_ln_gamma", "L0_attn_ln_beta",
          "L0_ffn_w_router", "L0_ffn_b_router", "L0_ffn_w_experts", "L0_ffn_b_experts")


def kernel(**inputs):
    import numpy as np
    import concourse.bacc as bacc
    from concourse.bass_utils import run_bass_kernel_spmd

    nc = bacc.Bacc("TRN2", target_bir_lowering=False, num_devices=1)
    arrays, args = {}, []
    for name in INPUTS:
        a = np.ascontiguousarray(inputs[name])
        arrays[name] = a
        args.append(nc.dram_tensor(name, a.shape, mybir.dt.from_np(a.dtype), kind="ExternalInput").ap())
    out = nc.dram_tensor("out", (BATCH, SEQ, D), F32, kind="ExternalOutput").ap()
    build(nc, *args, out)
    r = run_bass_kernel_spmd(nc, [arrays], core_ids=[0])
    return r.results[0]["out"]
```

```python
from contextlib import ExitStack

import concourse.bass as bass
import numpy as np
from concourse import mybir

F32 = mybir.dt.float32
F32R = mybir.dt.float32r
BF16 = mybir.dt.bfloat16
ALU = mybir.AluOpType
ACT = mybir.ActivationFunctionType
AX = mybir.AxisListType
ds = bass.ds

P = 128
BATCH, SEQ, D = 4, 1024, 256
TOK = BATCH * SEQ
NT = TOK // P
DK = D // P
NE = 8
HEADS, HD = 16, 16
CH = 512
TPC = CH // P
NCH = TOK // CH
EPS = 1e-5

GH = 4
HGS = HEADS // GH
NG = BATCH * HGS
KT = SEQ // P
SLOT = 32
SCALE = HD ** -0.5
MASKED = -1.0e30
ROWS = 6 * HD
MROWS = ROWS + 3
PARTS = ((0, 3), (3, 2), (5, 1))

EPIECES = NE * D // CH
WBANKS = 1 + EPIECES * DK

FIRST = (16, 23, 34, 35)

CREDIT = 8


def at(events):
    return max(events, 0) + CREDIT if isinstance(events, int) else events + CREDIT


class Group:

    def __init__(self, turn, u):
        self.turn, self.u = turn, u
        self.n = 3 * turn + u

    def __add__(self, k):
        return Group(self.turn + (self.u + k) // 3, (self.u + k) % 3)


class Signals:
    pass


class Shared:
    pass


def build(nc, x, w_qkv, w_proj, b_proj, ln_gamma, ln_beta, w_router, b_router, w_experts, b_experts, out):
    s = Shared()
    s.x_in = x.rearrange("b (t p) d -> p (b t) d", p=P)
    s.out = out.rearrange("b (t p) d -> p (b t) d", p=P)
    s.q_parts = nc.dram_tensor("q_parts", (3, D, TOK), BF16).ap()
    s.k_parts = nc.dram_tensor("k_parts", (3, D, TOK), BF16).ap()
    s.att_num = nc.dram_tensor("att_num", (D, TOK), F32).ap()
    s.att_rec = nc.dram_tensor("att_rec", (HEADS, TOK), F32).ap()
    s.w_qk = w_qkv[:, 0:2 * D].rearrange("(k p) n -> p k n", p=P)
    s.w_v = w_qkv[:, 2 * D:3 * D].rearrange("(k p) n -> p k n", p=P)
    s.w_proj = w_proj.rearrange("(k p) n -> p k n", p=P)
    s.w_experts = w_experts.rearrange("e (h p) d -> p (e h) d", p=P)
    s.w_router, s.b_router, s.b_experts = w_router, b_router.rearrange("(e a) -> e a", a=1), b_experts
    s.b_proj, s.ln_gamma, s.ln_beta = (row.rearrange("(a d) -> a d", a=1).broadcast_to([P, D])
                                       for row in (b_proj, ln_gamma, ln_beta))
    with ExitStack() as ctx:
        def sb(name, shape, dt=F32, scope=ctx):
            return scope.enter_context(nc.sbuf_tensor(name, shape, dt))

        s.xs = sb("xs", [P, NT, D])
        s.ln2 = sb("ln2", [P, NT, 2])
        s.ident = sb("ident", [P, P])
        s.ident_b = sb("ident_b", [P, P], BF16)
        s.eps = sb("eps", [P, 1])
        s.wp = sb("wp", [P, DK, D])
        s.gamma = sb("gamma", [P, D])
        s.beta = sb("beta", [P, D])
        s.bproj = sb("bproj", [P, D])
        s.brouter = sb("brouter", [NE, 1])
        s.before = sb("before", [P, TPC * NE, NE])
        s.wr = [sb(f"wr{n}", [P, DK, NE], F32R) for n in range(2)]
        s.we = [sb(f"we{n}", [P, DK, NE * D], F32R) for n in range(2)]
        s.bias_rows = sb("bias_rows", [P, TPC, D], BF16)
        s.v_at = nc.sbuf_base
        s.v_all = sb("v_all", [P, NT, D])
        s.behind_v = nc.sbuf_base
        s.banks = [ctx.enter_context(nc.psum_tensor(f"bank{n}", [P, CH], F32)) for n in range(8)]
        middle = attention(nc, s, ctx)
        front = ffn(nc, s, ctx, middle, True)
        back = ffn(nc, s, ctx, middle, False)
        with nc.Block() as block:
            @block.sync
            def _(sp):
                front.sync(sp)
                for one in back.every:
                    sp.sem_inc(one, CREDIT)
                back.sync(sp)

            @block.gpsimd
            def _(pool):
                front.gpsimd(pool)
                back.gpsimd(pool)

            @block.scalar
            def _(act):
                front.scalar(act)
                back.scalar(act)

            @block.tensor
            def _(pe):
                front.tensor(pe)
                back.tensor(pe)

            @block.vector
            def _(dve):
                front.vector(dve)
                back.vector(dve)


def ffn(nc, s, ctx, a, first):
    tag = "a" if first else "c"
    offset = s.behind_v if first else s.v_at

    def sb(name, shape, dt=F32):
        nonlocal offset
        here, size = offset, int(np.prod(shape[1:])) * (2 if dt == BF16 else 4)
        offset += -(-size // 32) * 32
        return nc.alloc_sbuf_tensor_at(f"{tag}_{name}", shape, dt, offset=here)

    every = []

    def sem(name):
        every.append(ctx.enter_context(nc.semaphore(f"{tag}_{name}")))
        return every[-1]

    q = Signals()
    if first:
        def once(name):
            return ctx.enter_context(nc.semaphore(name))

        q.x_in = [once(f"x_in{n}") for n in range(3)]
        q.experts_in = [once(f"experts_in{n}") for n in range(EPIECES)]
        q.router_in, q.bias_in, q.qk_in, q.v_in = once("router_in"), once("bias_in"), once("qk_in"), once("v_in")
        q.later_in = once("later_in")
        q.consts, q.bias_zero, q.bias_step, q.bias_placed = once("consts"), once("bias_zero"), once("bias_step"), once("bias_placed")
        q.w_turned, q.w_hi, q.w_lo, q.wqk_hi, q.wqk_lo = once("w_turned"), once("w_hi"), once("w_lo"), once("wqk_hi"), once("wqk_lo")
    q.normed_stats, q.normed_aggr, q.std_done = sem("normed_stats"), sem("normed_aggr"), sem("std_done")
    q.rstd_done, q.norm_ready, q.xh_ready = sem("rstd_done"), sem("norm_ready"), sem("xh_ready")
    q.turned, q.hi_ready, q.lo_ready = sem("turned"), sem("hi_ready"), sem("lo_ready")
    q.router_done, q.logits_ready, q.logits_turned = sem("router_done"), sem("logits_ready"), sem("logits_turned")
    q.logits_copied, q.rank_step, q.mask_ready = sem("logits_copied"), sem("rank_step"), sem("mask_ready")
    q.mask_zero, q.mask_turned, q.maskt_ready = sem("mask_zero"), sem("mask_turned"), sem("maskt_ready")
    q.bias_done, q.bias_ready = sem("bias_done"), sem("bias_ready")
    q.ffn_bank, q.combined, q.x_ready = sem("ffn_bank"), sem("combined"), sem("x_ready")
    q.apart = sem("apart")
    if first:
        q.st2, q.aggr2, q.std2, q.rstd2, q.norm2 = sem("st2"), sem("aggr2"), sem("std2"), sem("rstd2"), sem("norm2")
        q.xh2_ready, q.turned2, q.hi2_ready, q.lo2_ready = sem("xh2_ready"), sem("turned2"), sem("hi2_ready"), sem("lo2_ready")
        q.v_bank, q.v_ready, q.qk_bank = sem("v_bank"), sem("v_ready"), sem("qk_bank")
        q.qk_hi, q.qk_rest, q.qk_mid, q.qk_lo = sem("qk_hi"), sem("qk_rest"), sem("qk_mid"), sem("qk_lo")
        q.stored = s.qk_stored = [sem(f"stored{j}") for j in range(4)]
    else:
        q.num_loaded0, q.num_loaded1, q.att_ready = sem("num_loaded0"), sem("num_loaded1"), sem("att_ready")
        q.proj_bank, q.resid_ready, q.resid_bias, q.xa_ready = sem("proj_bank"), sem("resid_ready"), sem("resid_bias"), sem("xa_ready")
        q.st3, q.aggr3, q.std3, q.rstd3, q.norm3 = sem("st3"), sem("aggr3"), sem("std3"), sem("rstd3"), sem("norm3")
        q.y_ready, q.scaled, q.x_shifted, q.x2_ready = sem("y_ready"), sem("scaled"), sem("x_shifted"), sem("x2_ready")
        q.written = sem("written")

    if first:
        xt = [[sb(f"xt{par}{n}", [P, DK, CH], F32R) for n in range(2)] for par in range(2)]
        s.wqk = [sb(f"wqk{n}", [P, DK, 2 * D], F32R) for n in range(2)]
        s.wv = sb("wv", [P, DK, D])
    else:
        num = [sb(f"num{par}", [P, DK, CH]) for par in range(2)]
        rec = [sb(f"rec{par}", [P, DK, CH]) for par in range(2)]
        att = [sb(f"att{par}", [P, DK, CH]) for par in range(2)]
        resid = sb("resid", [P, TPC, D])
        residb = sb("residb", [P, TPC, D])
        xb = sb("xb", [P, TPC, D])
        xa = sb("xa", [P, TPC, D])
        yn = sb("yn", [P, TPC, D])
        yg = sb("yg", [P, TPC, D])
        st3, mv3, std3, ln3 = sb("st3", [P, TPC, 6]), sb("mv3", [P, TPC, 2]), sb("std3", [P, TPC, 1]), sb("ln3", [P, TPC, 2])
    st = sb("st", [P, TPC, 6])
    mv = sb("mv", [P, TPC, 2])
    std = sb("std", [P, TPC, 1])
    ln = sb("ln", [P, TPC, 2])
    xh = sb("xh", [P, TPC, D])
    if not first:
        xt = [[sb(f"xt0{n}", [P, DK, CH], F32R) for n in range(2)]]
    logits_t = sb("logits_t", [NE, CH])
    logits = sb("logits", [P, TPC * NE])
    gt = sb("gt", [P, TPC * NE, NE])
    eq = sb("eq", [P, TPC * NE, NE])
    wins = sb("wins", [P, TPC * NE, NE])
    rank = sb("rank", [P, TPC * NE])
    mask = [sb(f"mask{par}", [P, TPC, 32], BF16) for par in range(2)]
    mask_t = [sb(f"mask_t{par}", [P, P], BF16) for par in range(2)]
    if not first:
        xt.append([sb(f"xt1{n}", [P, DK, CH], F32R) for n in range(2)])
    ybias = [sb(f"ybias{pair}", [P, 2, D]) for pair in range(2)]
    acc = [[sb(f"acc{par}{n}", [P, D]) for n in range(2)] for par in range(2)]
    if first:
        ring, pb, pt, pr = [a.ms[2], a.es[2], *a.os], a.ms[1], a.es[0:2], a.ms[0]
    else:
        ring, pb, pt, pr = [*a.es, a.os[0]], a.os[1], a.ms[0:2], a.ms[2]
    pr_b = pr[:, 0:P // 2].bitcast(BF16)
    if first:
        we_in = s.v_all[:, 0:NE * DK, :]
        wqk_in = s.v_all[:, NE * DK:NE * DK + 2 * DK, :].rearrange("p (k a) d -> p k (a d)", k=DK)
        st2, mv2, std2 = sb("st2", [P, TPC, 6]), sb("mv2", [P, TPC, 2]), sb("std2", [P, TPC, 1])
        xh2 = sb("xh2", [P, TPC, D])
        xt2 = sb("xt2", [P, DK, CH])
        xt2r = [sb(f"xt2r{n}", [P, DK, CH], F32R) for n in range(2)]
        part = [sb(f"part{n}", [P, 3, CH], BF16) for n in range(4)]
        rest = [sb(f"rest{n}", [P, CH]) for n in range(2)]
        wr_in, be_in, be_rest = sb("wr_in", [NE, D]), sb("be_in", [NE, D]), sb("be_rest", [NE, D])
        be_part = sb("be_part", [NE, 3, D], BF16)
        unused = sb("unused", [P, 1])

    pairs = 2
    last_slot = NCH if first else NCH - 1

    def slots(engine, slot):
        slot(0, 0, 0)
        with engine.Fori(0, pairs) as i:
            for u in range(1, 3):
                slot(2 * i + u, u % 2, i + u // 2)
        for c in range(1 + 2 * pairs, last_slot + 1):
            slot(c, c % 2, c // 2)

    def takes_first(c, n):
        return first and isinstance(c, int) and c == NCH - 1 and n < FIRST[0] // TPC

    def exists(c):
        return not isinstance(c, int) or 0 <= c < NCH

    def tiles(c):
        return ds(TPC * c, TPC)

    def norm_stats(dve, src, m, st_, mv_, n_st, n_ag):
        for t in range(TPC):
            last = dve.bn_stats(st_[:, t, :], src(t))
        last.then_inc(n_st, 1)
        dve.wait_ge(n_st, at(m + 1))
        dve.sem_inc(q.apart, 1)
        for t in range(TPC):
            last = dve.bn_aggr(mv_[:, t, :], st_[:, t, :])
        last.then_inc(n_ag, 1)

    def norm_scale(dve, m, mv_, std_, out_ln, n_sd, n_rc, n_rd):
        dve.wait_ge(n_sd, at(m + 1))
        dve.reciprocal(out_ln[:, :, 0:1], std_[:]).then_inc(n_rc, 1)
        dve.wait_ge(n_rc, at(m + 1))
        dve.scalar_tensor_tensor(out=out_ln[:, :, 1:2], in0=mv_[:, :, 0:1], scalar=-1.0, in1=out_ln[:, :, 0:1],
                                 op0=ALU.mult, op1=ALU.mult).then_inc(n_rd, 1)

    def std_of(act, m, mv_, std_, n_ag, n_sd):
        act.wait_ge(n_ag, at(m + 1))
        act.activation(std_[:], mv_[:, :, 1:2], ACT.Sqrt, bias=s.eps[:, 0:1]).then_inc(n_sd, 1)

    def normalize(act, dst, src, ln_, done):
        for t in range(TPC):
            last = act.activation(dst[:, t, :], src(t), ACT.Identity, scale=ln_(t, 0), bias=ln_(t, 1))
        last.then_inc(done, 1)

    def row(c, t):
        return ds(TPC * c + t, 1)

    def xs_tile(m):
        return lambda t: s.xs[:, row(m, t), :].rearrange("p a d -> p (a d)")

    def ln2_of(m):
        return lambda t, n: s.ln2[:, row(m, t), n:n + 1].rearrange("p a b -> p (a b)")

    def transpose_chunk(dst, src):
        for h in range(DK):
            for t in range(TPC):
                last = nc.tensor.transpose(dst[h][:, t * P:(t + 1) * P], src[:, t, h * P:(h + 1) * P], s.ident[:])
        return last

    def pair_product(out_, w, wcols, xv, xcols, x_moves):
        steps = [(a, b, h) for h in range(DK) for a, b in ((0, 0), (0, 1), (1, 0))]
        for n, (a, b, h) in enumerate(steps):
            wa, xa_ = w[a][:, h, wcols], xv[b][:, h, xcols]
            last = nc.tensor.matmul(out_, wa if x_moves else xa_, xa_ if x_moves else wa,
                                    start=(n == 0), stop=(n == len(steps) - 1))
        return last

    def ring_wait(pe, c, i):
        if i >= 4:
            pe.wait_ge(q.combined, at(32 * c + 2 * (i - 3) if exists(c) else 32 * NCH))
            if not exists(c):
                pe.wait_ge(q.qk_rest, at(4 * (c - 2) + (i - 16) + 1))
        else:
            pe.wait_ge(q.combined, at(32 * (c - 1) + 2 * (13 + i)))
            if first:
                pe.wait_ge(q.qk_rest, at(4 * (c - 2) + i + 1))

    def sync(sp):
        if first:
            def load_x(n, lo, hi):
                sp.dma_start(s.xs[:, lo * TPC:hi * TPC, :], s.x_in[:, lo * TPC:hi * TPC, :]).then_inc(q.x_in[n], 16)

            load_x(0, 0, 1)
            per = NE * DK // EPIECES
            for n in range(EPIECES):
                sp.dma_start(we_in[:, n * per:(n + 1) * per, :],
                             s.w_experts[:, n * per:(n + 1) * per, :]).then_inc(q.experts_in[n], 16)
            load_x(1, 1, 2)
            for one in every + a.every:
                sp.sem_inc(one, CREDIT)

            sp.wait_ge(q.bias_zero, 1)
            sp.wait_ge(q.bias_step, 4)
            for t in range(TPC):
                for n in range(3):
                    at_row = 32 * t + NE * n
                    sp.dma_start(s.bias_rows[at_row:at_row + NE, t, :], be_part[:, n, :]).then_inc(q.bias_placed, 16)
            load_x(2, 2, NCH)
            sp.dma_start(s.wp[:], s.w_proj).then_inc(q.later_in, 16)
            sp.dma_start(s.bproj[:], s.b_proj).then_inc(q.later_in, 16)
            sp.dma_start(s.gamma[:], s.ln_gamma).then_inc(q.later_in, 16)
            sp.dma_start(s.beta[:], s.ln_beta).then_inc(q.later_in, 16)

        def load_attention(m, par):
            cols = ds(CH * m, CH)
            sp.wait_ge(q.att_ready, at(m - 1))
            loaded = (q.num_loaded0, q.num_loaded1)[par]
            sp.dma_start(num[par][:], s.att_num[:, cols].rearrange("(k p) n -> p k n", p=P)).then_inc(loaded, 16)
            for h in range(DK):
                rows = s.att_rec[h * KT:(h + 1) * KT, cols].unsqueeze(1).broadcast_to([KT, HD, CH])
                sp.dma_start(rec[par][:, h, :], rows).then_inc(loaded, 16)

        def store_parts(m):
            for j in range(4):
                dst = (s.q_parts, s.k_parts)[j // 2]
                sp.wait_ge(q.qk_lo, at(4 * m + j + 1))
                sp.dma_start(dst[:, (j % 2) * P:(j % 2 + 1) * P, ds(CH * m, CH)].rearrange("a p n -> p a n"),
                             part[j][:]).then_inc(q.stored[j], 16)

        def slot(c, par, nth):
            if first:
                if isinstance(c, int) and c == NCH:
                    sp.wait_ge(q.ffn_bank, at(16 * NCH))
                    a.load(sp, Group(0, 1))
                if isinstance(c, int) and c == NCH - 2:
                    for j in range(4):
                        sp.wait_ge(q.stored[j], at(16 * (SEQ // CH)))
                    a.load(sp, Group(0, 0))
                if exists(c - 1):
                    store_parts(c - 1)
            else:
                if exists(c + 3):
                    load_attention(c + 3, 1 - par)
                sp.wait_ge(q.x_ready, at(TPC * c + TPC))
                sp.dma_start(s.out[:, tiles(c), :], s.xs[:, tiles(c), :]).then_inc(q.written, 16)

        if not first:
            def lead(early, block):
                if (early, block) == (1, 0):
                    sp.wait_ge(a.v_copied, at(NG))
                    for u in range(3):
                        sp.wait_ge(a.stored[u], at(16 * GH * HGS))
                        sp.wait_ge(a.rec_stored[u], at(16 * GH * HGS))
                    load_attention(0, 0)
                    load_attention(1, 1)
                if (early, block) == (0, -1):
                    load_attention(2, 0)

            a.sync(sp, lead)
        slots(sp, slot)
        if first:
            sp.wait_ge(q.later_in, 16 * 4)
        else:
            sp.wait_ge(q.written, at(16 * NCH))

    def gpsimd(pool):
        if first:
            pool.memset(s.ident[:], 0.0).then_inc(q.consts, 1)
            pool.memset(s.before[:], 1.0).then_inc(q.consts, 1)
            pool.memset(s.eps[:], EPS).then_inc(q.consts, 1)
            pool.wait_ge(q.consts, 3)
            pool.affine_select(out=s.ident[:], in_=s.ident[:], compare_op=ALU.not_equal, fill=1.0, base=0,
                               pattern=[[-1, P]], channel_multiplier=1).then_inc(q.consts, 1)
            pool.memset(s.bias_rows[:], 0.0).then_inc(q.bias_zero, 1)
            before = s.before[:].rearrange("p (t e) f -> p t e f", e=NE)
            pool.affine_select(out=before, in_=before, compare_op=ALU.is_gt, fill=0.0, base=0,
                               pattern=[[0, TPC], [1, NE], [-1, NE]], channel_multiplier=0).then_inc(q.consts, 1)

        def clear_masks():
            for par in range(2):
                pool.memset(mask[par][:], 0.0).then_inc(q.mask_zero, 1)

        def add_tiles(c, which):
            for t in which:
                pool.wait_ge(q.combined, at(8 * (TPC * c + t) + 8))
                pool.sem_inc(q.apart, 1)
                pool.tensor_tensor(s.xs[:, row(c, t), :].rearrange("p a d -> p (a d)"), acc[t % 2][0][:],
                                   acc[t % 2][1][:], ALU.add).then_inc(q.x_ready, 1)

        def low_parts(m):
            for j in range(4):
                pool.wait_ge(q.qk_mid, at(4 * m + j + 1))
                pool.tensor_tensor(part[j][:, 2, :], rest[j % 2][:], part[j][:, 1, :],
                                   ALU.subtract).then_inc(q.qk_lo, 1)

        def add_bias(m):
            pool.wait_ge(q.resid_ready, at(m + 1))
            pool.wait_ge(q.xa_ready, at(2 * m))
            wide = s.bproj[:].unsqueeze(1).broadcast_to([P, TPC, D])
            pool.tensor_tensor(residb[:], resid[:], wide, ALU.add).then_inc(q.resid_bias, 1)

        def shift_x(m):
            pool.wait_ge(q.x2_ready, at(m))
            pool.sem_inc(q.apart, 1)
            pool.tensor_tensor(xb[:], s.xs[:, tiles(m), :], s.beta[:].unsqueeze(1).broadcast_to([P, TPC, D]),
                               ALU.add).then_inc(q.x_shifted, 1)

        def affine_add(m):
            pool.wait_ge(q.y_ready, at(m + 1))
            pool.tensor_tensor(yg[:], yn[:], s.gamma[:].unsqueeze(1).broadcast_to([P, TPC, D]),
                               ALU.mult).then_inc(q.scaled, 1)
            pool.wait_ge(q.scaled, at(m + 1))
            pool.wait_ge(q.x_shifted, at(m + 1))
            pool.sem_inc(q.apart, 1)
            pool.tensor_tensor(s.xs[:, tiles(m), :], yg[:], xb[:], ALU.add).then_inc(q.x2_ready, 1)

        def slot(c, par, nth):
            if first:
                if exists(c):
                    add_tiles(c, range(TPC))
                if exists(c - 1):
                    low_parts(c - 1)
                if isinstance(c, int) and c == NCH - 2:
                    a.ready_group0(pool)
            else:
                if exists(c + 2):
                    affine_add(c + 2)
                add_tiles(c, (0, 1))
                if exists(c + 3):
                    add_bias(c + 3)
                    shift_x(c + 3)
                add_tiles(c, (2, 3))

        if first:
            clear_masks()
        else:
            def lead(early, block):
                if (early, block) == (0, 1):
                    clear_masks()
                if (early, block) == (1, 4):
                    pool.wait_ge(a.expd, at(a.nexp * (NG - 2)))
                    shift_x(0)
                    add_bias(0)
                if (early, block) == (0, 3):
                    add_bias(1)
                if (early, block) == (0, 4):
                    shift_x(1)

            a.gpsimd(pool, lead)
            add_bias(2)
            shift_x(2)
        slots(pool, slot)
        if first:
            pool.wait_ge(q.qk_bank, at(4 * NCH))

    def scalar(act):
        def weights_hi(banks):
            for k in banks:
                act.wait_ge(q.w_turned, k + 1)
                if k == 0:
                    src, dst = ring[0][:, 0:DK * NE], s.wr[0][:].rearrange("p k e -> p (k e)")
                else:
                    n, half = divmod(k - 1, DK)
                    src, dst = ring[k % 4][:], s.we[0][:, half, n * CH:(n + 1) * CH]
                act.activation(dst, src, ACT.Copy).then_inc(q.w_hi, 1)

        def split_hi(m, par):
            act.wait_ge(q.turned, at(m + 1))
            act.wait_ge(q.ffn_bank, at(16 * (m - 1)))
            for h in range(DK):
                act.activation(xt[par][0][:, h, :], pt[h][:], ACT.Copy).then_inc(q.hi_ready, 1)

        def logits_out(m):
            act.wait_ge(q.router_done, at(m + 1))
            act.wait_ge(q.logits_turned, at(m))
            act.activation(logits_t[:], pr[0:NE, :], ACT.Identity, bias=s.brouter[:, 0:1]).then_inc(q.logits_ready, 1)

        def mask_out(m, par):
            act.wait_ge(q.mask_turned, at(m + 1))
            act.wait_ge(q.bias_done, at(2 * (m - 1)))
            act.activation(mask_t[par][:], pr_b[:], ACT.Copy).then_inc(q.maskt_ready, 1)

        def bias_out(c, pair):
            act.wait_ge(q.bias_done, at(2 * c + pair + 1))
            act.wait_ge(q.combined, at(8 * (TPC * (c - 1) + 2 * pair + 2)))
            act.activation(ybias[pair][:].rearrange("p t d -> p (t d)"), pb[:], ACT.Copy).then_inc(q.bias_ready, 1)

        def spread(m):
            std_of(act, m, mv, std, q.normed_aggr, q.std_done)

        def norm(m):
            act.wait_ge(q.norm_ready, at(m + 1))
            act.wait_ge(q.turned, at(m))
            act.sem_inc(q.apart, 1)
            normalize(act, xh, xs_tile(m), lambda t, n: ln[:, t, n:n + 1], q.xh_ready)

        def norm2(m):
            std_of(act, m, mv2, std2, q.aggr2, q.std2)
            act.wait_ge(q.norm2, at(m + 1))
            act.wait_ge(q.turned2, at(m))
            act.sem_inc(q.apart, 1)
            normalize(act, xh2, xs_tile(m), ln2_of(m), q.xh2_ready)

        def split2(m):
            act.wait_ge(q.turned2, at(m + 1))
            act.wait_ge(q.v_bank, at(2 * m))
            act.wait_ge(q.qk_bank, at(4 * m))
            act.wait_ge(q.lo2_ready, at(m))
            for h in range(DK):
                act.activation(xt2[:, h, :], pt[h][:], ACT.Copy)
                last = act.activation(xt2r[0][:, h, :], pt[h][:], ACT.Copy)
            last.then_inc(q.hi2_ready, 1)

        def v_out(m):
            for pair in range(2):
                act.wait_ge(q.v_bank, at(2 * m + pair + 1))
                act.sem_inc(q.apart, 1)
                act.activation(s.v_all[:, ds(TPC * m + 2 * pair, 2), :], pt[pair][:].rearrange("p (t d) -> p t d", d=D),
                               ACT.Copy).then_inc(q.v_ready, 1)

        def qk_hi(m, j):
            act.wait_ge(q.qk_bank, at(4 * m + j + 1))
            act.wait_ge(q.stored[j], at(16 * m))
            act.activation(part[j][:, 0, :], ring[j][:], ACT.Copy).then_inc(q.qk_hi, 1)

        def qk_mid(m, j):
            act.wait_ge(q.qk_rest, at(4 * m + j + 1))
            act.activation(part[j][:, 1, :], rest[j % 2][:], ACT.Copy).then_inc(q.qk_mid, 1)

        def residual(m):
            act.wait_ge(q.resid_bias, at(m))
            act.sem_inc(q.apart, 1)
            normalize(act, resid, xs_tile(m), ln2_of(m), q.resid_ready)

        def norm3(m):
            std_of(act, m, mv3, std3, q.aggr3, q.std3)
            act.wait_ge(q.norm3, at(m + 1))
            act.wait_ge(q.scaled, at(m))
            normalize(act, yn, lambda t: xa[:, t, :], lambda t, n: ln3[:, t, n:n + 1], q.y_ready)

        def slot(c, par, nth):
            if exists(c):
                bias_out(c, 0)
            if first and exists(c - 1):
                norm2(c - 1)
            if not first and exists(c + 2):
                norm3(c + 2)
            if exists(c + 1):
                split_hi(c + 1, 1 - par)
                logits_out(c + 1)
            if exists(c):
                bias_out(c, 1)
            if first and exists(c - 1):
                split2(c - 1)
                v_out(c - 1)
            if not first and exists(c + 3):
                residual(c + 3)
            if exists(c + 2):
                spread(c + 2)
            if exists(c + 1):
                mask_out(c + 1, 1 - par)
            if exists(c + 2):
                norm(c + 2)
            if first and exists(c - 1):
                for j in (0, 2):
                    qk_hi(c - 1, j)
                    qk_hi(c - 1, j + 1)
                    qk_mid(c - 1, j)
                    qk_mid(c - 1, j + 1)

        if first:
            act.dma_start(wr_in[:], s.w_router).then_inc(q.router_in, 16)
            act.dma_start(be_in[:], s.b_experts).then_inc(q.bias_in, 16)
            act.dma_start(s.brouter[:], s.b_router).then_inc(q.router_in, 16)
            act.dma_start(wqk_in, s.w_qk).then_inc(q.qk_in, 16)
            act.dma_start(s.wv[:], s.w_v).then_inc(q.v_in, 16)
            act.wait_ge(q.consts, 3)
            act.activation(unused[:], s.eps[:, 0:1], ACT.Sqrt)
            weights_hi((0,))
            spread(0)
            norm(0)
            weights_hi(range(1, 5))
            split_hi(0, 0)
            weights_hi(range(5, WBANKS))
            act.wait_ge(q.router_in, 2 * 16)
            act.sem_inc(q.apart, 1)
            logits_out(0)
            act.wait_ge(q.qk_in, 16)
            act.activation(s.wqk[0][:], wqk_in, ACT.Copy).then_inc(q.wqk_hi, 1)
            mask_out(0, 0)
            spread(1)
            norm(1)
        else:
            def lead(early, block):
                if (early, block) == (1, 6):
                    act.wait_ge(a.v_copied, at(NG))
                    residual(0)
                if (early, block) == (0, 2):
                    residual(1)
                if (early, block) == (0, 1):
                    std_of(act, 0, mv3, std3, q.aggr3, q.std3)
                if (early, block) == (0, 6):
                    std_of(act, 0, mv, std, q.normed_aggr, q.std_done)
                    std_of(act, 1, mv3, std3, q.aggr3, q.std3)
                if (early, block) == (0, 7):
                    split_hi(0, 0)
                if (early, block) == (0, 8):
                    logits_out(0)

            a.scalar(act, lead)
            mask_out(0, 0)
            spread(1)
            norm(1)
        slots(act, slot)
        if first:
            for j in range(4):
                act.wait_ge(q.stored[j], at(16 * NCH))

    def tensor(pe):
        def turn(m):
            pe.wait_ge(q.xh_ready, at(m + 1))
            if first:
                pe.wait_ge(q.v_ready, at(2 * (m - 2)))
            elif isinstance(m, int):
                pe.wait_ge(q.xa_ready, at(2 * min(m + 2, NCH)))
            else:
                pe.wait_ge(q.xa_ready, at(2 * (m + 2)))
            pe.wait_ge(q.lo_ready, at(2 * m))
            transpose_chunk(pt, xh).then_inc(q.turned, 1)

        def router(m, par):
            pe.wait_ge(q.lo_ready, at(2 * m + 2))
            pe.wait_ge(q.maskt_ready, at(m))
            pair_product(pr[0:NE, :], s.wr, slice(0, NE), xt[par], slice(0, CH), True).then_inc(q.router_done, 1)

        def turn_logits(m):
            pe.wait_ge(q.logits_ready, at(m + 1))
            pe.sem_inc(q.apart, 1)
            for t in range(TPC):
                last = nc.tensor.transpose(pr[:, t * NE:(t + 1) * NE], logits_t[:, t * P:(t + 1) * P],
                                           s.ident[0:NE, 0:NE])
            last.then_inc(q.logits_turned, 1)

        def turn_mask(m, par):
            pe.wait_ge(q.mask_ready, at(m + 1))
            nc.tensor.transpose(pr_b[:], mask[par][:].rearrange("p t e -> p (t e)"),
                                s.ident_b[:]).then_inc(q.mask_turned, 1)

        def bias(c, par, pair):
            pe.wait_ge(q.maskt_ready, at(c + 1))
            pe.wait_ge(q.bias_ready, at(2 * c + pair))
            for i in range(2):
                last = nc.tensor.matmul(pb[:, i * D:(i + 1) * D], mask_t[par][:], s.bias_rows[:, 2 * pair + i, :],
                                        start=True, stop=True)
            last.then_inc(q.bias_done, 1)

        def experts(c, par, t, which=range(4)):
            for n in which:
                ring_wait(pe, c, 4 * t + n)
                pair_product(ring[n][:], s.we, slice(n * CH, (n + 1) * CH), xt[par], slice(t * P, (t + 1) * P),
                             False).then_inc(q.ffn_bank, 1)
                if (t, n) == (TPC - 1, 2) and exists(c + 1):
                    turn_mask(c + 1, 1 - par)
                if takes_first(c, n):
                    if (t, n) == (0, 0):
                        pe.wait_ge(a.consts, at(2))
                        pe.wait_ge(q.maskt_ready, at(NCH))
                    a.first_scores(pe, FIRST[0] // TPC * t + n, FIRST[0] // TPC * t + n + 1)

        def turn2(m):
            pe.wait_ge(q.xh2_ready, at(m + 1))
            pe.wait_ge(q.lo_ready, at(2 * min(m + 3, NCH) if isinstance(m, int) else 2 * (m + 3)))
            pe.wait_ge(q.v_ready, at(2 * m))
            transpose_chunk(pt, xh2).then_inc(q.turned2, 1)

        def values(m):
            pe.wait_ge(q.hi2_ready, at(m + 1))
            for pair in range(2):
                for i in range(2):
                    for h in range(DK):
                        t = 2 * pair + i
                        last = nc.tensor.matmul(pt[pair][:, i * D:(i + 1) * D], xt2[:, h, t * P:(t + 1) * P],
                                                s.wv[:, h, :], start=(h == 0), stop=(h == DK - 1))
                last.then_inc(q.v_bank, 1)

        def queries_keys(m, c):
            pe.wait_ge(q.lo2_ready, at(m + 1))
            for j in range(4):
                ring_wait(pe, c, 16 + j)
                pair_product(ring[j][:], s.wqk, slice(j * P, (j + 1) * P), xt2r, slice(0, CH),
                             True).then_inc(q.qk_bank, 1)

        def project(m, par, pairs=(0, 1)):
            pe.wait_ge(q.att_ready, at(m + 1))
            pe.wait_ge(q.lo_ready, at(2 * (m - 1) if not isinstance(m, int) or m > 1 else 0))
            pe.wait_ge(q.xa_ready, at(2 * m))
            for pair in pairs:
                for i in range(2):
                    for h in range(DK):
                        t = 2 * pair + i
                        last = nc.tensor.matmul(pt[pair][:, i * D:(i + 1) * D], att[par][:, h, t * P:(t + 1) * P],
                                                s.wp[:, h, :], start=(h == 0), stop=(h == DK - 1))
                last.then_inc(q.proj_bank, 1)

        def slot(c, par, nth):
            if not first and exists(c + 2):
                project(c + 2, par)
            if first and isinstance(c, int) and c == 0:
                experts(0, 0, 0, (0, 1))
                turn_mask(0, 0)
                experts(0, 0, 0, (2,))
                pe.wait_ge(q.bias_placed, 16 * 3 * TPC)
                bias(0, 0, 0)
                experts(0, 0, 0, (3,))
                pe.wait_ge(q.v_in, 16)
                pe.wait_ge(q.wqk_lo, 1)
            elif exists(c):
                bias(c, par, 0)
                experts(c, par, 0)
            if exists(c + 1):
                turn(c + 1)
            if exists(c):
                experts(c, par, 1)
            if exists(c + 1):
                router(c + 1, 1 - par)
            if first and not exists(c):
                pe.wait_ge(q.bias_ready, at(2 * NCH))
                pe.wait_ge(q.qk_rest, at(4 * (NCH - 1)))
                a.first_scores(pe, FIRST[0], FIRST[1])
            if first and exists(c - 1):
                turn2(c - 1)
            if first and not exists(c):
                a.first_scores(pe, FIRST[1], FIRST[2])
            if exists(c):
                bias(c, par, 1)
                experts(c, par, 2)
            if exists(c + 1):
                turn_logits(c + 1)
            if first and exists(c - 1):
                values(c - 1)
            if first and not exists(c):
                a.first_scores(pe, FIRST[2], FIRST[3])
                pe.wait_ge(a.mread, at(FIRST[3]))
            if exists(c):
                experts(c, par, 3)
            if first and exists(c - 1):
                queries_keys(c - 1, c)

        def turn_weights(banks):
            for k in banks:
                if k >= 4:
                    pe.wait_ge(q.w_lo, k - 3)
                if k == 0:
                    pe.wait_ge(q.router_in, 2 * 16)
                    for h in range(DK):
                        last = nc.tensor.transpose(ring[0][:, h * NE:(h + 1) * NE], wr_in[:, h * P:(h + 1) * P],
                                                   s.ident[0:NE, 0:NE])
                else:
                    n, half = divmod(k - 1, DK)
                    pe.wait_ge(q.experts_in[n], 16)
                    for i in range(4):
                        last = nc.tensor.transpose(ring[k % 4][:, i * P:(i + 1) * P],
                                                   we_in[:, 4 * n + i, half * P:(half + 1) * P], s.ident[:])
                last.then_inc(q.w_turned, 1)

        if first:
            pe.wait_ge(q.consts, 4)
            turn_weights(range(5))
            turn(0)
            turn_weights(range(5, WBANKS))
            pe.wait_ge(q.w_lo, 1)
            router(0, 0)
            turn_logits(0)
            pe.wait_ge(q.w_lo, WBANKS)
        else:
            def lead(early, block):
                if (early, block) == (1, 10):
                    pe.wait_ge(a.mread, at(a.max_banks))
                    project(0, 0, (0,))
                if (early, block) == (1, 11):
                    project(0, 0, (1,))
                if (early, block) == (0, 3):
                    project(1, 1, (0,))
                    project(1, 1, (1,))
                if (early, block) == (0, 6):
                    turn(0)
                if (early, block) == (0, 8):
                    router(0, 0)
                if (early, block) == (0, 9):
                    turn_logits(0)

            a.tensor(pe, lead)
            turn_mask(0, 0)
            pe.wait_ge(a.expd, at(a.nexp * NG))
            pe.wait_ge(a.o_copied, at(2 * NG))
        slots(pe, slot)
        if first:
            pe.wait_ge(q.v_ready, at(2 * NCH))
            pe.wait_ge(q.qk_rest, at(4 * NCH))

    def vector(dve):
        def weights_lo(banks):
            for k in banks:
                dve.wait_ge(q.w_hi, k + 1)
                if k == 0:
                    src = ring[0][:, 0:DK * NE]
                    hi, lo = (w[:].rearrange("p k e -> p (k e)") for w in s.wr)
                else:
                    n, half = divmod(k - 1, DK)
                    src = ring[k % 4][:]
                    hi, lo = (w[:, half, n * CH:(n + 1) * CH] for w in s.we)
                dve.tensor_tensor(lo, src, hi.bitcast(F32), ALU.subtract).then_inc(q.w_lo, 1)

        def bias_parts():
            dve.wait_ge(q.bias_in, 16)
            dve.tensor_copy(be_part[:, 0, :], be_in[:]).then_inc(q.bias_step, 1)
            dve.wait_ge(q.bias_step, 1)
            dve.tensor_tensor(be_rest[:], be_in[:], be_part[:, 0, :], ALU.subtract).then_inc(q.bias_step, 1)
            dve.wait_ge(q.bias_step, 2)
            dve.tensor_copy(be_part[:, 1, :], be_rest[:]).then_inc(q.bias_step, 1)
            dve.wait_ge(q.bias_step, 3)
            dve.tensor_tensor(be_part[:, 2, :], be_rest[:], be_part[:, 1, :], ALU.subtract).then_inc(q.bias_step, 1)

        def norm(m):
            if first and isinstance(m, int) and m <= 2:
                dve.wait_ge(q.x_in[m], 16)
                dve.sem_inc(q.apart, 1)
            if not first:
                dve.wait_ge(q.x2_ready, at(m + 1))
                dve.sem_inc(q.apart, 1)
            norm_stats(dve, xs_tile(m), m, st, mv, q.normed_stats, q.normed_aggr)

        def scale(m):
            norm_scale(dve, m, mv, std, ln, q.std_done, q.rstd_done, q.norm_ready)

        def norm2(m):
            dve.wait_ge(q.x_ready, at(TPC * m + TPC))
            dve.sem_inc(q.apart, 1)
            norm_stats(dve, xs_tile(m), m, st2, mv2, q.st2, q.aggr2)
            norm_scale(dve, m, mv2, std2, s.ln2[:, tiles(m), :], q.std2, q.rstd2, q.norm2)

        def split_lo(m, par):
            for h in range(DK):
                dve.wait_ge(q.hi_ready, at(2 * m + h + 1))
                dve.tensor_tensor(xt[par][1][:, h, :], pt[h][:], xt[par][0][:, h, :].bitcast(F32),
                                  ALU.subtract).then_inc(q.lo_ready, 1)

        def split2(m):
            dve.wait_ge(q.hi2_ready, at(m + 1))
            dve.wait_ge(q.qk_bank, at(4 * m))
            dve.tensor_tensor(xt2r[1][:], xt2[:], xt2r[0][:].bitcast(F32), ALU.subtract).then_inc(q.lo2_ready, 1)

        def ranks(m, par):
            dve.wait_ge(q.logits_turned, at(m + 1))
            dve.tensor_copy(logits[:], pr[:, 0:TPC * NE]).then_inc(q.logits_copied, 1)
            dve.wait_ge(q.logits_copied, at(m + 1))
            other = logits[:].rearrange("p (t e) -> p t e", e=NE).unsqueeze(2).broadcast_to([P, TPC, NE, NE])
            own = logits[:].unsqueeze(2).broadcast_to([P, TPC * NE, NE])
            wide = lambda a: a[:].rearrange("p (t e) f -> p t e f", e=NE)
            own4 = own.rearrange("p (t e) f -> p t e f", e=NE)
            dve.tensor_tensor(wide(eq), other, own4, ALU.is_equal).then_inc(q.rank_step, 1)
            dve.tensor_tensor(wide(gt), other, own4, ALU.is_gt).then_inc(q.rank_step, 1)
            dve.wait_ge(q.rank_step, at(5 * m + 1))
            dve.tensor_tensor(wins[:], eq[:], s.before[:], ALU.mult).then_inc(q.rank_step, 1)
            dve.wait_ge(q.rank_step, at(5 * m + 3))
            dve.tensor_tensor(eq[:], wins[:], gt[:], ALU.add).then_inc(q.rank_step, 1)
            dve.wait_ge(q.rank_step, at(5 * m + 4))
            dve.tensor_reduce(rank[:], eq[:], AX.X, ALU.add).then_inc(q.rank_step, 1)
            dve.wait_ge(q.rank_step, at(5 * m + 5))
            dve.wait_ge(q.mask_zero, at(2))
            dve.wait_ge(q.mask_turned, at(m - 1))
            copies = rank[:].rearrange("p (t e) -> p t e", e=NE).unsqueeze(2).broadcast_to([P, TPC, 3, NE])
            dve.tensor_scalar(mask[par][:, :, 0:3 * NE].rearrange("p t (a e) -> p t a e", e=NE), copies,
                              2.0, 0.5, ALU.is_lt, ALU.mult).then_inc(q.mask_ready, 1)

        def combine(c, par, t):
            done = 8 * (TPC * c + t)
            for n in range(4):
                dve.wait_ge(q.ffn_bank, at(16 * c + 4 * t + n + 1))
                if n == 0:
                    dve.wait_ge(q.bias_ready, at(2 * c + t // 2 + 1))
                    dve.wait_ge(q.mask_ready, at(c + 1))
                    dve.wait_ge(q.x_ready, at(TPC * c + t - 1))
                for i in range(2):
                    dst = acc[t % 2][i]
                    if n:
                        dve.wait_ge(q.combined, at(done + 2 * (n - 1) + i + 1))
                        base = dst[:]
                    else:
                        base = (ybias[t // 2][:, t % 2, :], xs_tile(c)(t))[i]
                    dve.scalar_tensor_tensor(out=dst[:], in0=ring[n][:, i * D:(i + 1) * D],
                                             scalar=mask[par][:, t, 2 * n + i:2 * n + i + 1], in1=base,
                                             op0=ALU.mult, op1=ALU.add).then_inc(q.combined, 1)
                if takes_first(c, n):
                    a.first_reads(dve, FIRST[0] // TPC * t + n, FIRST[0] // TPC * t + n + 1)

        def qk_rests(m):
            for j in range(4):
                dve.wait_ge(q.qk_hi, at(4 * m + j + 1))
                dve.wait_ge(q.qk_lo, at(4 * m + j - 1))
                dve.tensor_tensor(rest[j % 2][:], ring[j][:], part[j][:, 0, :], ALU.subtract).then_inc(q.qk_rest, 1)

        def attended(m, par, nth):
            dve.wait_ge((q.num_loaded0, q.num_loaded1)[par], at(16 * 3 * (nth + 1)))
            dve.wait_ge(q.proj_bank, at(2 * (m - 1)))
            dve.tensor_tensor(att[par][:], num[par][:], rec[par][:], ALU.mult).then_inc(q.att_ready, 1)

        def add_residual(m):
            dve.wait_ge(q.resid_bias, at(m + 1))
            dve.wait_ge(q.y_ready, at(m))
            for pair in range(2):
                dve.wait_ge(q.proj_bank, at(2 * m + pair + 1))
                dve.tensor_tensor(xa[:, 2 * pair:2 * pair + 2, :], pt[pair][:].rearrange("p (t d) -> p t d", d=D),
                                  residb[:, 2 * pair:2 * pair + 2, :], ALU.add).then_inc(q.xa_ready, 1)
            dve.wait_ge(q.xa_ready, at(2 * m + 2))
            norm_stats(dve, lambda t: xa[:, t, :], m, st3, mv3, q.st3, q.aggr3)

        def scale3(m):
            norm_scale(dve, m, mv3, std3, ln3, q.std3, q.rstd3, q.norm3)

        def slot(c, par, nth):
            if first and exists(c - 1):
                norm2(c - 1)
            if first and not exists(c):
                a.first_reads(dve, FIRST[0], FIRST[1])
            if not first and exists(c + 2):
                add_residual(c + 2)
                scale3(c + 2)
            if exists(c):
                combine(c, par, 0)
            if exists(c + 1):
                split_lo(c + 1, 1 - par)
            if exists(c):
                combine(c, par, 1)
            if not first and exists(c + 3):
                attended(c + 3, 1 - par, nth + 1 + par)
            if exists(c):
                combine(c, par, 2)
            if exists(c + 1):
                ranks(c + 1, 1 - par)
            if first and exists(c - 1):
                split2(c - 1)
            if first and not exists(c):
                a.first_reads(dve, FIRST[1], FIRST[3])
            if exists(c + 2):
                norm(c + 2)
                scale(c + 2)
            if exists(c):
                combine(c, par, 3)
            if first and exists(c - 1):
                qk_rests(c - 1)

        if first:
            norm(0)
            bias_parts()
            scale(0)
            dve.wait_ge(q.consts, 5)
            dve.sem_inc(q.apart, 1)
            dve.tensor_copy(s.ident_b[:], s.ident[:]).then_inc(q.consts, 1)
            weights_lo(range(5))
            split_lo(0, 0)
            weights_lo(range(5, WBANKS))
            ranks(0, 0)
            dve.wait_ge(q.wqk_hi, 1)
            dve.tensor_tensor(s.wqk[1][:], wqk_in, s.wqk[0][:].bitcast(F32), ALU.subtract).then_inc(q.wqk_lo, 1)
            norm(1)
            scale(1)
        else:
            def scale_tiles(dst, src, ln_, done):
                for t in range(TPC):
                    last = dve.tensor_scalar(dst[:, t, :], src(t), ln_[:, t, 0:1], ln_[:, t, 1:2], ALU.mult, ALU.add)
                last.then_inc(done, 1)

            def sublayer(m):
                dve.wait_ge(q.norm3, at(m + 1))
                dve.wait_ge(q.x2_ready, at(m))
                dve.sem_inc(q.apart, 1)
                scale_tiles(yn, lambda t: xa[:, t, :], ln3, q.y_ready)
                dve.wait_ge(q.y_ready, at(m + 1))
                dve.tensor_tensor(yg[:], yn[:], s.gamma[:].unsqueeze(1).broadcast_to([P, TPC, D]),
                                  ALU.mult).then_inc(q.scaled, 1)
                dve.wait_ge(q.scaled, at(m + 1))
                dve.wait_ge(q.x_shifted, at(m + 1))
                dve.sem_inc(q.apart, 1)
                dve.tensor_tensor(s.xs[:, tiles(m), :], yg[:], xb[:], ALU.add).then_inc(q.x2_ready, 1)

            def lead(early, block):
                if (early, block) == (1, 23):
                    dve.wait_ge(a.v_copied, at(NG))
                    attended(0, 0, 0)
                    attended(1, 1, 0)
                if (early, block) == (0, 0):
                    add_residual(0)
                    scale3(0)
                    sublayer(0)
                    norm(0)
                    add_residual(1)
                    scale(0)
                    dve.wait_ge(q.norm_ready, at(1))
                    scale_tiles(xh, xs_tile(0), ln, q.xh_ready)
                    scale3(1)
                    sublayer(1)
                    split_lo(0, 0)
                    attended(2, 0, 1)
                    dve.wait_ge(q.resid_bias, at(2))
                    dve.sem_inc(q.apart, 1)
                    scale_tiles(resid, xs_tile(2), s.ln2[:, tiles(2), :], q.resid_ready)
                if (early, block) == (0, 2):
                    ranks(0, 0)
                    norm(1)
                    scale(1)

            a.vector(dve, lead)
        slots(dve, slot)

    f = Signals()
    f.every = every
    f.sync, f.gpsimd, f.scalar, f.tensor, f.vector = sync, gpsimd, scalar, tensor, vector
    return f


def query_blocks():
    for i in range(KT):
        for lo in range(0, (i + 1) * P, CH):
            width = min(CH, (i + 1) * P - lo)
            yield i, lo, width, CH // width, lo + width == (i + 1) * P


def key_blocks():
    for half in range(SEQ // CH):
        for j in range((half + 1) * CH // P):
            start = max(0, j * P - half * CH)
            yield j, half, start, CH - start


def max_units():
    return [(i, lo, width, range(c, c + hp), diagonal) for i, lo, width, hp, diagonal in query_blocks()
            for c in range(0, GH, hp)]


def exp_units():
    return [[range(c, c + CH // width) for c in range(0, GH, CH // width)] for _, _, _, width in key_blocks()]


def attention(nc, s, ctx):
    keys = list(key_blocks())
    eunits = exp_units()
    munits = max_units()
    nexp = sum(len(u) for u in eunits)
    nmax = len(munits) + 1
    early = 14
    nkb = len(keys)
    half_blocks = CH // P
    assert nmax % 3 == 0
    offset = s.behind_v

    def sb(name, shape, dt=F32):
        nonlocal offset
        here, size = offset, int(np.prod(shape[1:])) * (2 if dt == BF16 else 4)
        offset += -(-size // 32) * 32
        return nc.alloc_sbuf_tensor_at(f"b_{name}", shape, dt, offset=here)

    a = Signals()
    a.every = every = []

    def sem(name):
        every.append(ctx.enter_context(nc.semaphore(f"b_{name}")))
        return every[-1]

    assert (NG - 1) % 3 == 0
    qs, ks, vs = [None] * 3, [None] * 3, [None] * 3
    for u in (1, 2):
        qs[u], ks[u] = sb(f"qs{u}", [MROWS, GH, SEQ], BF16), sb(f"ks{u}", [MROWS, GH, SEQ], BF16)
    for u in (1, 2):
        vs[u] = sb(f"vs{u}", [P, KT, GH, SLOT])
    probs = [sb(f"probs{n}", [P, GH, CH]) for n in range(3)]
    oev = [sb(f"oev{u}", [P, SEQ]) for u in range(3)]
    den = [sb(f"den{u}", [P, SEQ // SLOT]) for u in range(3)]
    rcp = [sb(f"rcp{u}", [P, SEQ // SLOT]) for u in range(3)]
    turned = sb("turned", [GH * KT, P])
    turned_rest = sb("turned_rest", [GH * KT, P])
    mparts = [sb(f"mparts{u}", [GH * KT, 3, P], BF16) for u in range(3)]
    vs[0] = sb("vs0", [P, KT, GH, SLOT])
    qs[0], ks[0] = sb("qs0", [MROWS, GH, SEQ], BF16), sb("ks0", [MROWS, GH, SEQ], BF16)
    neg1 = [sb(f"neg1{u}", [P, GH, KT]) for u in range(3)]
    neg2 = [sb(f"neg2{u}", [P, GH, KT - CH // P]) for u in range(3)]
    masked_b = sb("masked_b", [P, P], BF16)
    a.es = es = s.banks[0:3]
    a.ms = ms = s.banks[3:6]
    a.os = os_ = s.banks[6:8]

    consts, vones = sem("consts"), sem("vones")
    loaded = [sem(f"loaded{u}") for u in range(3)]
    mplaced = [sem(f"mplaced{u}") for u in range(3)]
    stored = [sem(f"stored{u}") for u in range(3)]
    den_placed = [sem(f"den_placed{u}") for u in range(3)]
    mscore, mread = sem("mscore"), sem("mread")
    mfinal, mpart = sem("mfinal"), sem("mpart")
    escore, expd, kept, summed = sem("escore"), sem("expd"), sem("kept"), sem("summed")
    apart = sem("apart")
    rec_stored = [sem(f"rec_stored{u}") for u in range(3)]
    v_copied, o_copied, inverted = sem("v_copied"), sem("o_copied"), sem("inverted")

    def slots(engine, slot):
        slot(Group(0, 0))
        with engine.Fori(0, (NG - 4) // 3) as i:
            for u in range(1, 4):
                slot(Group(i, 0) + u)
        for g in range(NG - 3, NG):
            slot(Group(0, 0) + g)

    def exists(g):
        return not isinstance(g.n, int) or 0 <= g.n < NG

    def lead_step(lead, g, block):
        if isinstance(g.n, int) and g.n >= NG - 2:
            lead(NG - 1 - g.n, block)

    def stream(g):
        rest = [(g + 1, n) for n in range(early, len(munits))] if exists(g + 1) else []
        new = [(g + 2, n) for n in range(early)] if exists(g + 2) else []
        turn = [(g + 1, None)] if exists(g + 1) else []
        return rest + new[:3] + turn + new[3:]

    first_stream = ([(Group(0, 0), n) for n in range(len(munits))] + [(Group(0, 1), n) for n in range(3)] + [(Group(0, 0), None)]
                    + [(Group(0, 1), n) for n in range(3, early)])

    def place(g, n):
        return nmax + early + nmax * g.n + n, (early + n) % 3

    def exp_bank(g, unit):
        return (nexp * g.u + unit) % 3

    unit0 = [sum(len(u) for u in eunits[:b]) for b in range(nkb + 1)]
    sel_blocks = [b for b, (j, half, start, width) in enumerate(keys) if half * CH + start == j * P]

    def load(sp, g):
        sp.wait_ge(escore, at(nexp * (g.n - 2)))
        head, tok = (g.n % HGS) * (GH * HD), (g.n // HGS) * SEQ
        for part, (piece, reps) in enumerate(PARTS):
            rows = slice(piece * HD, (piece + reps) * HD)
            q_src = s.q_parts[part, ds(head, GH * HD), ds(tok, SEQ)].rearrange("(c r) n -> r c n", r=HD)
            for a in range(reps):
                sp.dma_start(qs[g.u][(piece + a) * HD:(piece + a + 1) * HD, :, :], q_src).then_inc(loaded[g.u], 16)
                k_src = s.k_parts[a, ds(head, GH * HD), ds(tok, SEQ)].rearrange("(c r) n -> r c n", r=HD)
                sp.dma_start(ks[g.u][(piece + a) * HD:(piece + a + 1) * HD, :, :], k_src).then_inc(loaded[g.u], 16)

    def copy_values(pool, g):
        src = s.v_all[:, ds((g.n // HGS) * KT, KT), ds((g.n % HGS) * (GH * HD), GH * HD)]
        pool.tensor_copy(vs[g.u][:, :, :, 0:HD], src.rearrange("p j (c r) -> p j c r", r=HD)).then_inc(v_copied, 1)

    def ones(pool, u):
        pool.memset(vs[u][:, :, :, HD:SLOT], 1.0).then_inc(vones, 1)
        pool.wait_ge(vones, at(2 * u + 1))
        pool.memset(ks[u][ROWS:MROWS, :, :], 1.0).then_inc(vones, 1)
        pool.wait_ge(vones, at(2 * u + 2))

    def ready_group0(pool):
        pool.memset(masked_b[:], 0.0).then_inc(consts, 1)
        pool.wait_ge(consts, at(1))
        pool.affine_select(out=masked_b[:], in_=masked_b[:], compare_op=ALU.is_ge, fill=MASKED, base=0,
                           pattern=[[-1, P]], channel_multiplier=1).then_inc(consts, 1)
        pool.wait_ge(consts, at(2))
        ones(pool, 0)
        copy_values(pool, Group(0, 0))

    def max_scores(pe, entry, position, bank):
        g, n = entry
        pe.wait_ge(mread, at(position - 2))
        if n is None:
            pe.wait_ge(mfinal, at(g.n + 1))
            nc.tensor.transpose(ms[bank][0:GH * KT, 0:P], neg1[g.u][:].rearrange("p c i -> p (c i)"),
                                s.ident[:]).then_inc(mscore, 1)
            return
        if n == 0:
            pe.wait_ge(loaded[g.u], at(16 * 12 * (g.turn + 1)))
        i, lo, width, heads, diagonal = munits[n]
        for a, c in enumerate(heads):
            last = nc.tensor.matmul(ms[bank][:, a * width:(a + 1) * width], qs[g.u][0:ROWS, c, i * P:(i + 1) * P],
                                    ks[g.u][0:ROWS, c, lo:lo + width], start=True, stop=not diagonal)
            if diagonal:
                last = nc.tensor.matmul(ms[bank][:, (a + 1) * width - P:(a + 1) * width], s.ident_b[:],
                                        masked_b[:], start=False, stop=True)
        last.then_inc(mscore, 1)

    def max_read(dve, entry, position, bank):
        g, n = entry
        dve.wait_ge(mscore, at(position + 1))
        if n is None:
            t, r, m = turned, turned_rest, mparts[g.u]
            dve.tensor_copy(t[:], ms[bank][0:GH * KT, 0:P]).then_inc(mread, 1)
            dve.wait_ge(mread, at(position + 1))
            if not (isinstance(g.turn, int) and g.turn == 0):
                dve.wait_ge(mplaced[g.u], at(16 * 3 * g.turn))
            dve.tensor_copy(m[:, 0, :], t[:]).then_inc(mpart, 1)
            dve.wait_ge(mpart, at(5 * g.n + 1))
            dve.tensor_tensor(r[:], t[:], m[:, 0, :], ALU.subtract).then_inc(mpart, 1)
            dve.wait_ge(mpart, at(5 * g.n + 2))
            dve.tensor_copy(m[:, 1, :], r[:]).then_inc(mpart, 1)
            dve.wait_ge(mpart, at(5 * g.n + 3))
            dve.tensor_tensor(m[:, 2, :], r[:], m[:, 1, :], ALU.subtract).then_inc(mpart, 2)
            return
        i, lo, width, heads, diagonal = munits[n]
        dst = neg1[g.u][:, heads[0]:heads[0] + len(heads), i:i + 1] if lo == 0 else \
            neg2[g.u][:, heads[0]:heads[0] + len(heads), i - CH // P:i - CH // P + 1]
        dve.tensor_reduce(dst, ms[bank][:, 0:len(heads) * width].rearrange("p (h w) -> p h w", w=width), AX.X,
                          ALU.max, negate=True).then_inc(mread, 1)
        if n == len(munits) - 1:
            dve.wait_ge(mread, at(position + 1))
            late = neg1[g.u][:, :, CH // P:KT]
            dve.tensor_tensor(late, late, neg2[g.u][:], ALU.min).then_inc(mfinal, 1)

    def first_bank(position):
        return 0 if position < FIRST[0] else position % 3

    def first_scores(pe, lo, hi):
        for position in range(lo, hi):
            if position < FIRST[0]:
                pe.wait_ge(mread, at(position))
            max_scores(pe, first_stream[position], position, first_bank(position))

    def first_reads(dve, lo, hi):
        for position in range(lo, hi):
            max_read(dve, first_stream[position], position, first_bank(position))

    def sync(sp, lead):
        def place_maxima(g):
            sp.wait_ge(mpart, at(5 * g.n + 5))
            for part in range(3):
                sp.dma_start(qs[g.u][ROWS + part:ROWS + part + 1, :, :].rearrange("a c n -> a (c n)"),
                             mparts[g.u][:, part, :]).then_inc(mplaced[g.u], 16)

        def store(g):
            head, tok = (g.n % HGS) * (GH * HD), (g.n // HGS) * SEQ
            sp.wait_ge(o_copied, at(2 * g.n + 2))
            for c in range(GH):
                sp.dma_start(s.att_num[ds(head + c * HD, HD), ds(tok, SEQ)],
                             oev[g.u][SLOT * c:SLOT * c + HD, :]).then_inc(stored[g.u], 16)
                sp.dma_start(den[g.u][SLOT * c:SLOT * (c + 1), :],
                             oev[g.u][SLOT * c + HD:SLOT * c + HD + 1, :]).then_inc(den_placed[g.u], 16)

        def store_inverse(g):
            tok = (g.n // HGS) * SEQ
            sp.wait_ge(inverted, at(g.n + 1))
            for c in range(GH):
                dst = s.att_rec[ds((g.n % HGS) * GH + c, 1), ds(tok, SEQ)].rearrange("a (p n) -> (a p) n", p=SLOT)
                sp.dma_start(dst, rcp[g.u][SLOT * c:SLOT * (c + 1), :]).then_inc(rec_stored[g.u], 16)

        place_maxima(Group(0, 0))
        for one in s.qk_stored:
            sp.wait_ge(one, at(16 * NCH))

        def slot(g):
            if exists(g + 2):
                load(sp, g + 2)
            lead_step(lead, g, -1)
            if exists(g + (-1)):
                store(g + (-1))
            lead_step(lead, g, 0)
            if exists(g + (-1)):
                store_inverse(g + (-1))
            if exists(g + 1):
                place_maxima(g + 1)

        slots(sp, slot)
        store(Group(0, 0) + (NG - 1))
        store_inverse(Group(0, 0) + (NG - 1))
        for u in range(3):
            sp.wait_ge(stored[u], at(16 * GH * len(range(u, NG, 3))))
            sp.wait_ge(rec_stored[u], at(16 * GH * len(range(u, NG, 3))))

    def gpsimd(pool, lead):
        for u in (1, 2):
            ones(pool, u)

        def slot(g):
            for b, (j, half, start, width) in enumerate(keys):
                if b in sel_blocks:
                    pool.wait_ge(expd, at(nexp * g.n + unit0[b + 1]))
                    pool.sem_inc(apart, 1)
                    part = probs[b % 3][:, :, 0:P]
                    pool.affine_select(out=part, in_=part, compare_op=ALU.is_ge, fill=0.0, base=0,
                                       pattern=[[0, GH], [1, P]], channel_multiplier=-1).then_inc(kept, 1)
                if b == 4 and exists(g + 1):
                    pool.wait_ge(summed, at(nkb * (g.n - 1)))
                    copy_values(pool, g + 1)
                lead_step(lead, g, b)

        slots(pool, slot)

    def scalar(act, lead):
        def copy_out(g, half):
            act.wait_ge(summed, at(nkb * g.n + (4 if half == 0 else nkb)))
            if isinstance(g.turn, int) and g.turn == 0:
                pass
            else:
                act.wait_ge(stored[g.u], at(16 * GH * g.turn))
                act.wait_ge(den_placed[g.u], at(16 * GH * g.turn))
            act.activation(oev[g.u][:, half * CH:(half + 1) * CH], os_[half][:], ACT.Copy).then_inc(o_copied, 1)

        def slot(g):
            for b, (j, half, start, width) in enumerate(keys):
                for n, heads in enumerate(eunits[b]):
                    unit = unit0[b] + n
                    act.wait_ge(escore, at(nexp * g.n + unit + 1))
                    if n == 0:
                        act.wait_ge(summed, at(nkb * g.n + b - 2))
                    hp = len(heads)
                    act.activation(probs[b % 3][:, heads[0]:heads[0] + hp, 0:width],
                                   es[exp_bank(g, unit)][:, 0:hp * width].rearrange("p (h w) -> p h w", w=width),
                                   ACT.Exp, scale=SCALE).then_inc(expd, 1)
                if b == 1 and exists(g + (-1)):
                    copy_out(g + (-1), 1)
                if b == 5:
                    copy_out(g, 0)
                lead_step(lead, g, b)

        slots(act, slot)
        copy_out(Group(0, 0) + (NG - 1), 1)

    def tensor(pe, lead):
        def exp_unit(g, b, n):
            j, half, start, width = keys[b]
            unit = unit0[b] + n
            if unit == 0:
                pe.wait_ge(mplaced[g.u], at(16 * 3 * (g.turn + 1)))
            pe.wait_ge(expd, at(nexp * g.n + unit - 2))
            for a, c in enumerate(eunits[b][n]):
                first_q = half * CH + start
                last = nc.tensor.matmul(es[exp_bank(g, unit)][:, a * width:(a + 1) * width],
                                        ks[g.u][:, c, j * P:(j + 1) * P], qs[g.u][:, c, first_q:first_q + width],
                                        start=True, stop=True)
            last.then_inc(escore, 1)

        def products(g, b):
            j, half, start, width = keys[b]
            pe.wait_ge(expd, at(nexp * g.n + unit0[b + 1]))
            if b in sel_blocks:
                pe.wait_ge(kept, at(len(sel_blocks) * g.n + sel_blocks.index(b) + 1))
            if b == 0:
                pe.wait_ge(v_copied, at(g.n + 1))
            if j == 0:
                pe.wait_ge(o_copied, at(2 * g.n - 1 + half))
            for c in range(GH):
                last = nc.tensor.matmul(os_[half][SLOT * c:SLOT * (c + 1), start:CH], vs[g.u][:, j, c, :],
                                        probs[b % 3][:, c, 0:width], start=(j == 0),
                                        stop=(j == (half + 1) * CH // P - 1))
            last.then_inc(summed, 1)

        first_scores(pe, FIRST[-1], len(first_stream))
        pe.wait_ge(vones, at(6))

        def slot(g):
            lead_step(lead, g, -1)
            entries = list(enumerate(stream(g)))
            for b in range(nkb):
                for n in range(len(eunits[b])):
                    exp_unit(g, b, n)
                    while entries and entries[0][0] < unit0[b] + n:
                        at, entry = entries.pop(0)
                        max_scores(pe, entry, *place(g, at))
                    if (b, n) == (0, 1) and exists(g + (-1)):
                        products(g + (-1), nkb - 2)
                    if (b, n) == (half_blocks, 1):
                        products(g, half_blocks - 2)
                if b == 0 and exists(g + (-1)):
                    products(g + (-1), nkb - 1)
                if b > 0 and b not in (half_blocks - 1, nkb - 1):
                    products(g, b - 1)
                lead_step(lead, g, b)
            for at, entry in entries:
                max_scores(pe, entry, *place(g, at))

        slots(pe, slot)
        products(Group(0, 0) + (NG - 1), nkb - 2)
        products(Group(0, 0) + (NG - 1), nkb - 1)

    def vector(dve, lead):
        first_reads(dve, FIRST[-1], len(first_stream))

        def invert(g):
            dve.wait_ge(den_placed[g.u], at(16 * GH * (g.turn + 1)))
            dve.wait_ge(rec_stored[g.u], at(16 * GH * g.turn))
            dve.reciprocal(rcp[g.u][:], den[g.u][:]).then_inc(inverted, 1)

        def slot(g):
            for at, entry in enumerate(stream(g)):
                max_read(dve, entry, *place(g, at))
                if at == 16 and exists(g + (-1)):
                    invert(g + (-1))
                lead_step(lead, g, at)
            if not stream(g):
                lead_step(lead, g, 0)
            if not stream(g) and exists(g + (-1)):
                invert(g + (-1))

        slots(dve, slot)
        lead(0, 2)
        invert(Group(0, 0) + (NG - 1))

    a.nexp, a.v_copied, a.mread, a.expd, a.o_copied, a.stored, a.rec_stored = nexp, v_copied, mread, expd, o_copied, stored, rec_stored
    a.max_banks = place(Group(0, 0) + (NG - 2), len(stream(Group(0, 0) + (NG - 2))) - 1)[0] + 1
    a.v_read, a.load, a.ready_group0, a.first_scores, a.first_reads = v_copied, load, ready_group0, first_scores, first_reads
    a.consts = consts
    a.sync, a.gpsimd, a.scalar, a.tensor, a.vector = sync, gpsimd, scalar, tensor, vector
    return a


INPUTS = ("L0_attn_target", "L0_attn_w_qkv", "L0_attn_w_proj", "L0_attn_b_proj", "L0_attn_ln_gamma", "L0_attn_ln_beta",
          "L0_ffn_w_router", "L0_ffn_b_router", "L0_ffn_w_experts", "L0_ffn_b_experts")


def kernel(**inputs):
    import numpy as np
    import concourse.bacc as bacc
    from concourse.bass_utils import run_bass_kernel_spmd

    nc = bacc.Bacc("TRN2", target_bir_lowering=False, num_devices=1)
    arrays, args = {}, []
    for name in INPUTS:
        a = np.ascontiguousarray(inputs[name])
        arrays[name] = a
        args.append(nc.dram_tensor(name, a.shape, mybir.dt.from_np(a.dtype), kind="ExternalInput").ap())
    out = nc.dram_tensor("out", (BATCH, SEQ, D), F32, kind="ExternalOutput").ap()
    build(nc, *args, out)
    r = run_bass_kernel_spmd(nc, [arrays], core_ids=[0])
    return r.results[0]["out"]
```
